# Optimizing a Trainium2 kernel written in Bass

```python
import numpy as np
import jax
import jax.numpy as jnp

def _softmax(x, axis=-1):
    return jax.nn.softmax(x, axis=axis)

def _gelu(x):
    return jax.nn.gelu(x, approximate=True)

def _silu(x):
    return jax.nn.silu(x)

def _sigmoid(x):
    return jax.nn.sigmoid(x)

def _layernorm(x, axis=-1, eps=1e-05):
    m = jnp.mean(x, axis=axis, keepdims=True)
    v = jnp.var(x, axis=axis, keepdims=True)
    return (x - m) / jnp.sqrt(v + eps)

def _scatter_add(tgt, idx, src, axis=0):
    return tgt.at[idx].add(src)

def _segment_sum(src, seg, n):
    return jax.ops.segment_sum(src, seg, n)
kernel_name = 'mk_seq_preln_d1_jaxref_r4_ef20d3'

def setup_inputs(seed: int=0):
    np.random.seed(seed)
    _w = jnp.asarray

    def _L0_attn_setup():
        import jax, jax.numpy as jnp
        import numpy as np
        B, L, DM, ED, N, R, K = (2, 256, 256, 512, 16, 64, 4)
        key = jax.random.key(seed)
        ks = jax.random.split(key, 8)
        s = 0.02
        x = jax.random.normal(ks[0], (B, L, DM), jnp.float32)
        in_proj_w = jax.random.normal(ks[1], (2 * ED, DM), jnp.float32) * s
        conv_w = jax.random.normal(ks[2], (ED, 1, K), jnp.float32) * 0.3
        x_proj_w = jax.random.normal(ks[3], (R + 2 * N, ED), jnp.float32) * s
        dt_proj_w = jax.random.normal(ks[4], (ED, R), jnp.float32) * R ** (-0.5)
        dt_proj_b = jax.random.uniform(ks[5], (ED,), jnp.float32, minval=-4.6, maxval=-2.3)
        A_log = jnp.log(jnp.tile(jnp.arange(1, N + 1, dtype=jnp.float32), (ED, 1)))
        D = jnp.ones((ED,), jnp.float32)
        out_proj_w = jax.random.normal(ks[6], (DM, ED), jnp.float32) * s
        return dict(x=x, in_proj_w=in_proj_w, conv_w=conv_w, x_proj_w=x_proj_w, dt_proj_w=dt_proj_w, dt_proj_b=dt_proj_b, A_log=A_log, D=D, out_proj_w=out_proj_w)
    _L0_attn_in = _L0_attn_setup()

    def _L0_ffn_setup():
        import jax, jax.numpy as jnp
        import numpy as np
        D_MODEL = 256
        EXPERT_DIM = 128
        N_EXPERTS = 8
        TOP_K = 2

        def _sq_relu(h):
            return jnp.square(jax.nn.relu(h))
        key = jax.random.key(seed)
        ks = jax.random.split(key, 6)
        s = 0.02
        x = jax.random.normal(ks[0], (2, 512, D_MODEL), dtype=jnp.float32)
        Ws1 = jax.random.normal(ks[1], (D_MODEL, EXPERT_DIM), dtype=jnp.float32) * s
        Ws2 = jax.random.normal(ks[2], (EXPERT_DIM, D_MODEL), dtype=jnp.float32) * s
        W1 = jax.random.normal(ks[3], (N_EXPERTS, D_MODEL, EXPERT_DIM), dtype=jnp.float32) * s
        W2 = jax.random.normal(ks[4], (N_EXPERTS, EXPERT_DIM, D_MODEL), dtype=jnp.float32) * s
        Wr = jax.random.normal(ks[5], (D_MODEL, N_EXPERTS), dtype=jnp.float32) * s
        return {'x': x, 'Ws1': Ws1, 'Ws2': Ws2, 'W1': W1, 'W2': W2, 'Wr': Wr}
    _L0_ffn_in = _L0_ffn_setup()
    _d = {'L0_attn_x': _L0_attn_in['x'], 'L0_attn_in_proj_w': _L0_attn_in['in_proj_w'], 'L0_attn_conv_w': _L0_attn_in['conv_w'], 'L0_attn_x_proj_w': _L0_attn_in['x_proj_w'], 'L0_attn_dt_proj_w': _L0_attn_in['dt_proj_w'], 'L0_attn_dt_proj_b': _L0_attn_in['dt_proj_b'], 'L0_attn_A_log': _L0_attn_in['A_log'], 'L0_attn_D': _L0_attn_in['D'], 'L0_attn_out_proj_w': _L0_attn_in['out_proj_w'], 'L0_ffn_Ws1': _L0_ffn_in['Ws1'], 'L0_ffn_Ws2': _L0_ffn_in['Ws2'], 'L0_ffn_W1': _L0_ffn_in['W1'], 'L0_ffn_W2': _L0_ffn_in['W2'], 'L0_ffn_Wr': _L0_ffn_in['Wr']}
    _x0 = _d['L0_attn_x']
    _d['L0_attn_x'] = jax.random.normal(jax.random.fold_in(jax.random.key(seed), 1), (8, 1024, 256), dtype=_x0.dtype)
    del _x0
    return _d

def reference(L0_attn_x, L0_attn_in_proj_w, L0_attn_conv_w, L0_attn_x_proj_w, L0_attn_dt_proj_w, L0_attn_dt_proj_b, L0_attn_A_log, L0_attn_D, L0_attn_out_proj_w, L0_ffn_Ws1, L0_ffn_Ws2, L0_ffn_W1, L0_ffn_W2, L0_ffn_Wr):

    def _L0_attn_ref(x, in_proj_w, conv_w, x_proj_w, dt_proj_w, dt_proj_b, A_log, D, out_proj_w):
        import jax, jax.numpy as jnp
        import numpy as np
        B, L, DM, ED, N, R, K = (2, 256, 256, 512, 16, 64, 4)
        xz = jnp.einsum('bld,ed->ble', x, in_proj_w)
        xp, z = (xz[..., :ED], xz[..., ED:])
        xc = jax.lax.conv_general_dilated(xp.transpose(0, 2, 1), conv_w, window_strides=(1,), padding=[(K - 1, 0)], feature_group_count=ED, dimension_numbers=('NCH', 'OIH', 'NCH'))
        xc = jax.nn.silu(xc.transpose(0, 2, 1))
        dBC = jnp.einsum('ble,fe->blf', xc, x_proj_w)
        dt, Bm, Cm = (dBC[..., :R], dBC[..., R:R + N], dBC[..., R + N:])
        delta = jax.nn.softplus(jnp.einsum('blr,er->ble', dt, dt_proj_w) + dt_proj_b)
        A = -jnp.exp(A_log)
        dA = jnp.exp(delta[..., None] * A)
        BX = delta[..., None] * Bm[:, :, None, :] * xc[..., None]

        def comb(c1, c2):
            a1, b1 = c1
            a2, b2 = c2
            return (a1 * a2, b1 * a2 + b2)
        _, hs = jax.lax.associative_scan(comb, (dA, BX), axis=1)
        y = jnp.einsum('blen,bln->ble', hs, Cm) + D * xc
        out = jnp.einsum('ble,de->bld', y * jax.nn.silu(z), out_proj_w)
        return out

    def _L0_ffn_ref(x, Ws1, Ws2, W1, W2, Wr):
        import jax, jax.numpy as jnp
        import numpy as np
        D_MODEL = 256
        EXPERT_DIM = 128
        N_EXPERTS = 8
        TOP_K = 2

        def _sq_relu(h):
            return jnp.square(jax.nn.relu(h))
        shape = x.shape
        xf = x.reshape(-1, D_MODEL)
        out_shared = _sq_relu(xf @ Ws1) @ Ws2
        logits = xf @ Wr
        top_vals, top_idx = jax.lax.top_k(logits, TOP_K)
        rw = jax.nn.softmax(top_vals.astype(jnp.float32), axis=-1).astype(x.dtype)
        onehot = jax.nn.one_hot(top_idx, N_EXPERTS, dtype=x.dtype)
        prob = jnp.einsum('tk,tke->te', rw, onehot)
        prob = jnp.trunc(prob)
        h = _sq_relu(jnp.einsum('td,edf->tef', xf, W1))
        y = jnp.einsum('tef,efd->ted', h, W2)
        out_routed = jnp.einsum('ted,te->td', y, prob)
        return (out_shared + out_routed).reshape(shape)
    x = L0_attn_x
    x = x + _L0_attn_ref(_layernorm(x, axis=-1), L0_attn_in_proj_w, L0_attn_conv_w, L0_attn_x_proj_w, L0_attn_dt_proj_w, L0_attn_dt_proj_b, L0_attn_A_log, L0_attn_D, L0_attn_out_proj_w)
    x = x + _L0_ffn_ref(_layernorm(x, axis=-1), L0_ffn_Ws1, L0_ffn_Ws2, L0_ffn_W1, L0_ffn_W2, L0_ffn_Wr)
    return x

_drawn_inputs = setup_inputs


def setup_inputs(seed=0):
    import zlib

    import numpy as np

    out = dict(_drawn_inputs(seed))
    spreads = {'L0_attn_D': (1.0, 0.2)}
    factors = {}
    for name, (base, spread) in spreads.items():
        noise = np.random.default_rng([zlib.crc32(name.encode()), seed]).standard_normal(out[name].shape)
        drawn = base * np.exp(spread * noise) if base else spread * noise
        out[name] = jnp.asarray(drawn.astype(out[name].dtype))
    for name, factor in factors.items():
        out[name] = (out[name] * factor).astype(out[name].dtype)
    return out
```

```python
from contextlib import ExitStack

import concourse.bass as bass
from concourse import mybir

F32 = mybir.dt.float32
BF16 = mybir.dt.bfloat16
I32 = mybir.dt.int32
ALU = mybir.AluOpType
ACT = mybir.ActivationFunctionType

P = 128
CH = 512
EPS = 1e-5


class Track:

    def __init__(self, sem, amount=1):
        self.sem, self.amount, self.names, self.at = sem, amount, {}, 0
        self.closed = False

    def mark(self, name):
        if name in self.names:
            if self.names[name] == 1:
                self.closed = True
                self.at = 0
            assert self.names[name] == self.at + 1, (name, self.names[name], self.at)
        else:
            assert not self.closed, name
            self.names[name] = self.at + 1
        self.at += 1

    def value(self, name, seq):
        if isinstance(seq, int) and seq < 0:
            return None
        return (seq * len(self.names) + self.names[name]) * self.amount


def mamba_moe(nc, x, in_wT, conv_w, x_wT, dt_wT, dt_b, A_log, D, out_wT, Ws1, Ws2, W1, W2, Wr, out):
    NB, L, DM = x.shape
    ED = out_wT.shape[0]
    N = A_log.shape[1]
    K = conv_w.shape[2]
    R = dt_wT.shape[0]
    F = Ws1.shape[1]
    NE = Wr.shape[1]
    G = ED // P
    KD = DM // P
    TB = CH // P
    HV = L // CH
    NQ = NB * HV
    FX = R + 2 * N
    NG2 = G // 2
    STEPS = NG2 * N
    assert HV == 2 and KD == 2 and FX == 96 and N == 16 and F == P

    x_v = x.rearrange("b (h t p) d -> (b h) p t d", h=HV, p=P)
    out_v = out.rearrange("b (h t p) d -> (b h) p t d", h=HV, p=P)
    c_dram = nc.dram_tensor("c_scratch", (HV, N, CH), F32, kind="Internal").ap()
    x2_dram = nc.dram_tensor("x2_scratch", (NQ, P, KD, CH), F32, kind="Internal").ap()

    with ExitStack() as ctx:
        def sb(name, shape, dt=F32):
            return ctx.enter_context(nc.sbuf_tensor(name, shape, dt))

        def pb(name):
            return ctx.enter_context(nc.psum_tensor(name, [P, 512], F32))

        def sem(name):
            return ctx.enter_context(nc.semaphore(name))

        w_in = sb("w_in", [P, KD, 2 * ED])
        w_conv = sb("w_conv", [P, G, K])
        w_diag = sb("w_diag", [P, G, K, P])
        w_x = sb("w_x", [P, G, FX])
        w_dt = sb("w_dt", [FX, ED])
        b_dt = sb("b_dt", [P, G])
        a_log = sb("a_log", [P, G, N])
        a_neg = sb("a_neg", [P, G, N])
        d_skip = sb("d_skip", [P, G])
        w_out = sb("w_out", [P, G, DM])
        w_s1 = sb("w_s1", [P, KD, F])
        w_s2 = sb("w_s2", [P, DM])
        w_r = sb("w_r", [P, KD, NE])
        ident = sb("ident", [P, P])
        sel = sb("sel", [FX, N, P], BF16)
        mhalf = sb("mhalf", [P, TB])
        xt = sb("xt", [P, TB, DM])
        xn = sb("xn", [P, TB, DM])
        st = sb("st", [P, TB, 6])
        mv = sb("mv", [P, TB, 2])
        ve = sb("ve", [P, TB])
        rstd = sb("rstd", [P, TB])
        xnT = sb("xnT", [P, KD, CH])
        xp = sb("xp", [P, G, K - 1 + CH])
        xc = [sb(f"xc{h}", [P, G, CH]) for h in range(HV)]
        gate = [sb(f"gate{h}", [P, G, CH]) for h in range(HV)]
        delta = [sb(f"delta{h}", [P, G, CH]) for h in range(HV)]
        u = [sb(f"u{h}", [P, G, CH]) for h in range(HV)]
        dbc = sb("dbc", [FX, CH])
        bc_hi = sb("bc_hi", [FX, CH], BF16)
        bc_mid = sb("bc_mid", [FX, CH], BF16)
        bc_r = sb("bc_r", [FX, CH])
        bc3 = [sb(f"bc3_{h}", [FX, CH], BF16) for h in range(HV)]
        cb = sb("cb", [P, N, CH])
        bx = [sb(f"bx{i}", [P, 2, CH]) for i in range(2)]
        hs = [sb(f"hs{i}", [P, 2, CH]) for i in range(2)]
        hc = [sb(f"hc{i}", [P, 2, CH]) for i in range(2)]
        hlast = sb("hlast", [P, STEPS, 2])
        x1 = sb("x1", [P, TB, DM])
        x2n = sb("x2n", [P, TB, DM])
        st2 = sb("st2", [P, TB, 6])
        mv2 = sb("mv2", [P, TB, 2])
        ve2 = sb("ve2", [P, TB])
        rstd2 = sb("rstd2", [P, TB])
        x2T = sb("x2T", [P, KD, CH])
        hT = sb("hT", [P, CH])
        lg = sb("lg", [P, TB, NE])
        top8 = sb("top8", [P, TB, 8])
        gap = sb("gap", [P, TB])
        p_top = sb("p_top", [P, TB])
        is_top = sb("is_top", [P, TB, NE])
        prob = sb("prob", [P, NQ, TB, NE])
        any_p = sb("any_p", [P, 1])
        ones = sb("ones", [P, 1])
        flag = sb("flag", [1, 1], I32)
        Y = [pb("Y0"), pb("Y1")]
        BB = [pb("BB0"), pb("BB1")]
        DA = [pb("DA0"), pb("DA1")]
        PA, PB = pb("PA"), pb("PB")

        s_w = sem("s_w")
        s_g = sem("s_g")
        s_v0 = sem("s_v0")
        s_a0 = sem("s_a0")
        T = {
            "bb": Track(sem("m_bb")), "da": Track(sem("m_da")), "bx": Track(sem("m_bx")),
            "sc": Track(sem("m_sc")), "hl": Track(sem("m_hl")), "hc": Track(sem("m_hc")),
            "y": Track(sem("m_y")),
            "px": Track(sem("p_x"), 16), "pt": Track(sem("p_t")), "pv": Track(sem("p_v")),
            "pa": Track(sem("p_a")), "pg": Track(sem("p_g")),
            "pc": Track(sem("p_c"), 16), "cb": Track(sem("p_cb"), 16),
            "qx": Track(sem("q_x"), 16), "qt": Track(sem("q_t")), "qv": Track(sem("q_v")),
            "qa": Track(sem("q_a")), "qg": Track(sem("q_g")), "qo": Track(sem("q_o"), 16),
            "q2": Track(sem("q_x2"), 16),
            "ri": Track(sem("r_in"), 16), "ra": Track(sem("r_acc"), 16), "ro": Track(sem("r_out"), 16),
            "rt": Track(sem("r_t")), "rs": Track(sem("r_a")), "rv": Track(sem("r_v")),
        }
        where = {}

        queues = {}
        q = None

        s_carry = {"V": sem("carry_v"), "G": sem("carry_g"), "S": sem("carry_s")}

        def op(engine, make, after=(), done=None, r=0, carrier=False):
            if done:
                T[done[0]].mark((done[1], r % HV))
                where[done[1]] = T[done[0]]

            def run(e, b):
                for name, c in after:
                    track = where[name]
                    v = track.value((name, c % HV), b + c // HV)
                    if v is not None:
                        e.wait_ge(track.sem, v)
                        if engine == "S" and not isinstance(v, int):
                            e.sem_inc(s_carry[engine], 1)
                if carrier and engine != "S" and after and not isinstance(b, int):
                    e.sem_inc(s_carry[engine], 1)
                ins = make(e, b)
                if done:
                    ins.then_inc(T[done[0]].sem, T[done[0]].amount)
            q.setdefault(engine, []).append(run)

        def chunk(b, r):
            return b * HV + r

        def layernorm(pre, r, src, dst, stt, mvt, vet, rt, ready, freed):
            tv, tg = pre + "v", pre + "g"
            for t in range(TB):
                op("V", lambda e, b, t=t: e.bn_stats(stt[:, t, :], src[:, t, :]),
                   after=ready if t == 0 else (), done=(tv, f"{pre}_st{t}"), r=r)
            for t in range(TB):
                w = [(f"{pre}_st{t}", r)]
                if t == 0:
                    w.append((f"{pre}_ve", r - 1))
                op("V", lambda e, b, t=t: e.bn_aggr(mvt[:, t, :], stt[:, t, :]),
                   after=w, done=(tv, f"{pre}_mv{t}"), r=r, carrier=True)
            op("G", lambda e, b: e.tensor_scalar(vet[:, :], mvt[:, :, 1], EPS, None, ALU.add),
               after=[(f"{pre}_mv{TB - 1}", r), (f"{pre}_rstd", r - 1)], done=(tg, f"{pre}_ve"), r=r, carrier=True)
            op("G", lambda e, b: e.tensor_tensor(rt[:, :], vet[:, :], mhalf[:, :], ALU.pow),
               after=[(f"{pre}_ve", r), (f"{pre}_n{TB - 1}", r - 1)], done=(tg, f"{pre}_rstd"), r=r)
            for t in range(TB):
                op("V", lambda e, b, t=t: e.tensor_scalar(
                    dst[:, t, :], src[:, t, :], mvt[:, t, 0:1], rt[:, t:t + 1], ALU.subtract, ALU.mult),
                   after=([(f"{pre}_rstd", r)] + freed) if t == 0 else (), done=(tv, f"{pre}_n{t}"), r=r)

        def transposed(pre, k, r, src, dst, bank, freed, bank_free):
            for t in range(TB):
                op("T", lambda e, b, t=t: e.transpose(
                    bank[:, t * P:(t + 1) * P], src[:, t, k * P:(k + 1) * P], ident[:, :]),
                   after=[(f"{pre}_n{t}", r)] + (bank_free if t == 0 else []),
                   done=(pre + "t", f"{pre}_tr{k}") if t == TB - 1 else None, r=r)
            op("A", lambda e, b: e.activation(dst[:, k, :], bank[:, :], ACT.Copy),
               after=[(f"{pre}_tr{k}", r)] + freed, done=(pre + "a", f"{pre}_trc{k}"), r=r)

        def prep_load(r):
            op("S", lambda e, b: e.dma_start(xt[:, :, :], x_v[chunk(b, r)]),
               after=[(f"p_n{TB - 1}", r - 1)], done=("px", "x"), r=r, carrier=True)

        def prep_norm(r):
            layernorm("p", r, xt, xn, st, mv, ve, rstd, [("x", r)], [("p_tr1", r - 1)])

        def prep_transpose(r, k):
            bank_free = [("dt3", r - 1)] if k == 0 else [("p_trc0", r)]
            transposed("p", k, r, xn, xnT, PA, [("z3_mm", r - 1)], bank_free)

        def prep_halo(r):
            halo = xp[:, :, 0:K - 1]
            if r % HV == 0:
                op("A", lambda e, b: e.activation(
                    halo, halo0[:, :, :], ACT.Copy),
                   after=[("cv3_mm", r - 1), ("halo", r - 1)], done=("pa", "halo"), r=r)
            else:
                op("A", lambda e, b: e.activation(halo, xp[:, :, CH:CH + K - 1], ACT.Copy),
                   after=[("cv3_mm", r - 1), ("xp3", r - 1)], done=("pa", "halo"), r=r)

        def prep_in(r, g):
            for k in range(KD):
                op("T", lambda e, b, k=k: e.matmul(PA[:, :], w_in[:, k, g * P:(g + 1) * P], xnT[:, k, :],
                                                   start=(k == 0), stop=(k == KD - 1)),
                   after=[("p_trc1" if g == 0 else f"xp{g - 1}", r)] if k == 0 else (),
                   done=("pt", f"xp{g}_mm") if k == KD - 1 else None, r=r)
            op("A", lambda e, b: e.activation(xp[:, g, K - 1:], PA[:, :], ACT.Copy),
               after=[(f"xp{g}_mm", r), ("halo", r)], done=("pa", f"xp{g}"), r=r)

        def prep_z(r, g):
            for k in range(KD):
                op("T", lambda e, b, k=k: e.matmul(
                    PA[:, :], w_in[:, k, ED + g * P:ED + (g + 1) * P], xnT[:, k, :],
                    start=(k == 0), stop=(k == KD - 1)),
                   after=[("xp3" if g == 0 else f"z{g - 1}", r)] if k == 0 else (),
                   done=("pt", f"z{g}_mm") if k == KD - 1 else None, r=r)
            op("A", lambda e, b: e.activation(gate[r % HV][:, g, :], PA[:, :], ACT.Copy),
               after=[(f"z{g}_mm", r), ("op1_mm", r - 2)], done=("pa", f"z{g}"), r=r)

        def prep_conv(r, g):
            for k in range(K):
                op("T", lambda e, b, k=k: e.matmul(PA[:, :], w_diag[:, g, k, :], xp[:, g, k:k + CH],
                                                   start=(k == 0), stop=(k == K - 1)),
                   after=[("z3" if g == 0 else f"cv{g - 1}", r)] if k == 0 else (),
                   done=("pt", f"cv{g}_mm") if k == K - 1 else None, r=r)
            op("A", lambda e, b: e.activation(xc[r % HV][:, g, :], PA[:, :], ACT.Copy),
               after=[(f"cv{g}_mm", r), ("yg1", r - 2)], done=("pa", f"cv{g}"), r=r)

        def prep_silu(r):
            h = r % HV
            op("A", lambda e, b: e.activation(xc[h][:, :, :], xc[h][:, :, :], ACT.Silu),
               after=[("cv3", r)], done=("pa", "xc"), r=r)
            op("A", lambda e, b: e.activation(gate[h][:, :, :], gate[h][:, :, :], ACT.Silu),
               after=[("z3", r)], done=("pa", "gate"), r=r)

        def prep_x(r):
            h = r % HV
            lo, hi = FX - 2 * N, FX
            for g in range(G):
                op("T", lambda e, b, g=g: e.matmul(PA[0:FX, :], w_x[:, g, :], xc[h][:, g, :],
                                                   start=(g == 0), stop=(g == G - 1)),
                   after=[("xc", r)] if g == 0 else (),
                   done=("pt", "xw_mm") if g == G - 1 else None, r=r)
            op("A", lambda e, b: e.activation(dbc[:, :], PA[0:FX, :], ACT.Copy),
               after=[("xw_mm", r), ("dt3_mm", r - 1), ("b_r", r - 1), ("c_out", r - 1)],
               done=("pa", "dbc"), r=r)
            op("S", lambda e, b: e.dma_start(c_dram[h], dbc[R + N:FX, :]),
               after=[("dbc", r), (f"cb{N // 4 - 1}", r - 2)], done=("pc", "c_out"), r=r)
            op("A", lambda e, b: e.activation(bc_hi[lo:hi, :], dbc[lo:hi, :], ACT.Copy),
               after=[("dbc", r)], done=("pa", "b_hi"), r=r)
            op("A", lambda e, b: e.activation(bc3[h][0:32, :], dbc[lo:hi, :], ACT.Copy),
               after=[(f"bb{STEPS - 1}", r - 2)], done=("pa", "b_hi0"), r=r)
            op("V", lambda e, b: e.tensor_tensor(bc_r[lo:hi, :], dbc[lo:hi, :], bc_hi[lo:hi, :], ALU.subtract),
               after=[("b_hi", r), ("b_mid0", r - 1)], done=("pv", "b_r"), r=r)
            op("A", lambda e, b: e.activation(bc_mid[lo:hi, :], bc_r[lo:hi, :], ACT.Copy),
               after=[("b_r", r)], done=("pa", "b_mid"), r=r)
            op("A", lambda e, b: e.activation(bc3[h][32:64, :], bc_r[lo:hi, :], ACT.Copy),
               after=(), done=("pa", "b_mid0"), r=r)
            op("V", lambda e, b: e.tensor_tensor(bc3[h][lo:hi, :], bc_r[lo:hi, :], bc_mid[lo:hi, :], ALU.subtract),
               after=[("b_mid", r), (f"bb{STEPS - 1}", r - 2)], done=("pv", "b_lo"), r=r)

        def prep_dt(r, g):
            h = r % HV
            op("T", lambda e, b: e.matmul(PA[:, :], w_dt[:, g * P:(g + 1) * P], dbc[:, :], start=True, stop=True),
               after=[("dbc" if g == 0 else f"dt{g - 1}", r)], done=("pt", f"dt{g}_mm"), r=r)
            op("A", lambda e, b: e.activation(delta[h][:, g, :], PA[:, :], ACT.Identity, bias=b_dt[:, g:g + 1]),
               after=[(f"dt{g}_mm", r), (f"da{STEPS - 1}_1", r - 2), ("u", r - 2)], done=("pa", f"dt{g}"), r=r)

        def prep_softplus(r):
            h = r % HV
            op("A", lambda e, b: e.activation(u[h][:, :, :], delta[h][:, :, :], ACT.Abs),
               after=[("dt3", r), (f"bx{STEPS - 1}", r - 2)], done=("pa", "sp0"), r=r)
            op("A", lambda e, b: e.activation(u[h][:, :, :], u[h][:, :, :], ACT.Exp, scale=-1.0),
               after=[("sp0", r)], done=("pa", "sp1"), r=r)
            op("A", lambda e, b: e.activation(u[h][:, :, :], u[h][:, :, :], ACT.Ln, bias=1.0),
               after=[("sp1", r)], done=("pa", "sp2"), r=r)
            op("V", lambda e, b: e.scalar_tensor_tensor(out=delta[h][:, :, :], in0=delta[h][:, :, :], scalar=0.0,
                                                        in1=u[h][:, :, :], op0=ALU.max, op1=ALU.add),
               after=[("sp2", r)], done=("pv", "delta"), r=r)
            op("V", lambda e, b: e.tensor_tensor(u[h][:, :, :], delta[h][:, :, :], xc[h][:, :, :], ALU.mult),
               after=[("delta", r), ("xc", r)], done=("pv", "u"), r=r)

        def prep_cb(r, j):
            h = r % HV
            op("S", lambda e, b: e.dma_start(cb[:, 4 * j:4 * j + 4, :],
                                             c_dram[h, 4 * j:4 * j + 4, :].partition_broadcast(P)),
               after=[("c_out", r), (f"hc{STEPS - N + 4 * j + 3}", r - 1)]
               + ([(f"cb{j - 1}", r)] if j else [(f"cb{N // 4 - 1}", r - 1)]),
               done=("cb", f"cb{j}"), r=r)

        def before(s, r, d):
            s -= d
            return (s, r) if s >= 0 else (s + STEPS, r - 1)

        def after_step(name, s, r, d, tail=""):
            s, r = before(s, r, d)
            return (f"{name}{s}{tail}", r)

        def main_bcast(s, r):
            op("T", lambda e, b: e.matmul(BB[s % 2][:, :], sel[:, s % N, :], bc3[r % HV][:, :],
                                          start=True, stop=True),
               after=[after_step("bx", s, r, 2)] + ([("b_lo", r), ("b_mid0", r)] if s == 0 else []),
               done=("bb", f"bb{s}"), r=r)

        def main_exp(s, r):
            pair, n = divmod(s, N)
            for g in range(2):
                gg = 2 * pair + g
                op("A", lambda e, b, g=g, gg=gg: e.activation(
                    DA[g][:, :], delta[r % HV][:, gg, :], ACT.Exp, scale=a_neg[:, gg, n:n + 1]),
                   after=[after_step("sc", s, r, 1, f"_{g}")] + ([("delta", r)] if s == 0 else []),
                   done=("da", f"da{s}_{g}"), r=r)

        def main_scan(s, r):
            pair, n = divmod(s, N)
            h = r % HV
            op("V", lambda e, b: e.tensor_tensor(
                bx[s % 2][:, :, :], u[h][:, 2 * pair:2 * pair + 2, :],
                BB[s % 2][:, :].rearrange("p (o t) -> p o t", o=1).broadcast_to([P, 2, CH]), ALU.mult),
               after=[(f"bb{s}", r), after_step("sc", s, r, 2, "_1")] + ([("u", r)] if s == 0 else []),
               done=("bx", f"bx{s}"), r=r)
            for g in range(2):
                first = 0.0 if h == 0 else hlast[:, s, g:g + 1]
                wait = [(f"da{s}_{g}", r)]
                if g == 0:
                    wait += [(f"bx{s}", r), after_step("hc", s, r, 2)]
                    if h:
                        wait.append((f"hl{s}", r - 1))
                op("V", lambda e, b, g=g, first=first: e.tensor_tensor_scan(
                    hs[s % 2][:, g, :], DA[g][:, :], bx[s % 2][:, g, :], first, ALU.mult, ALU.add),
                   after=wait, done=("sc", f"sc{s}_{g}"), r=r)
            if h == 0:
                op("V", lambda e, b: e.tensor_copy(hlast[:, s, :], hs[s % 2][:, :, CH - 1]),
                   after=[(f"sc{s}_1", r)], done=("hl", f"hl{s}"), r=r)

        def main_times_c(s, r):
            n = s % N
            op("G", lambda e, b: e.tensor_tensor(
                hc[s % 2][:, :, :], hs[s % 2][:, :, :],
                cb[:, n:n + 1, :].broadcast_to([P, 2, CH]), ALU.mult),
               after=[(f"sc{s}_1", r)] + [after_step("y", s, r, 2)]
               + ([(f"cb{n // 4}", r)] if s < N and n % 4 == 0 else []),
               done=("hc", f"hc{s}"), r=r)

        def main_sum(s, r):
            n = s % N
            for g in range(2):
                w = []
                if g == 0:
                    w.append((f"hc{s}", r))
                    if n == 0:
                        w.append(("yd0", r) if s else ("yd1", r - 1))
                op("T", lambda e, b, g=g: e.matmul(Y[g][:, :], ident[:, :], hc[s % 2][:, g, :],
                                                   start=(n == 0), stop=(n == N - 1)),
                   after=w, done=("y", f"y{s}") if g else None, r=r)

        def post_gate(r, pair):
            h = r % HV
            for g in range(2):
                gg = 2 * pair + g
                op("V", lambda e, b, g=g, gg=gg: e.scalar_tensor_tensor(
                    out=xc[h][:, gg, :], in0=xc[h][:, gg, :], scalar=d_skip[:, gg:gg + 1], in1=Y[g][:, :],
                    op0=ALU.mult, op1=ALU.add),
                   after=[(f"y{pair * N + N - 1}", r)] if g == 0 else (),
                   done=("qv", f"yd{pair}" if g else f"yd{pair}_"), r=r)
            pr = slice(2 * pair, 2 * pair + 2)
            op("V", lambda e, b: e.tensor_tensor(gate[h][:, pr, :], gate[h][:, pr, :], xc[h][:, pr, :], ALU.mult),
               after=[(f"yd{pair}", r), ("gate", r)], done=("qv", f"yg{pair}"), r=r)

        def post_load(r):
            op("S", lambda e, b: e.dma_start(x1[:, :, :], x_v[chunk(b, r)]),
               after=[("o", r - 1)], done=("qx", "xr"), r=r, carrier=True)

        def post_out(r, k):
            h = r % HV
            for t2 in range(2):
                t = 2 * k + t2
                for g in range(G):
                    w = []
                    if t2 == 0 and g == 0:
                        w = [("yg0", r), ("yg1", r), ("x1_0", r) if k else ("o1", r - 1)]
                    op("T", lambda e, b, t=t, t2=t2, g=g: e.matmul(
                        PB[:, t2 * DM:(t2 + 1) * DM], gate[h][:, g, t * P:(t + 1) * P], w_out[:, g, :],
                        start=(g == 0), stop=(g == G - 1)),
                       after=w, done=("qt", f"op{k}_mm") if t2 == 1 and g == G - 1 else None, r=r)
            op("V", lambda e, b: e.tensor_tensor(
                x1[:, 2 * k:2 * k + 2, :], x1[:, 2 * k:2 * k + 2, :],
                PB[:, :].rearrange("p (t d) -> p t d", t=2), ALU.add),
               after=[(f"op{k}_mm", r), ("xr", r)], done=("qv", f"x1_{k}"), r=r)

        def post_norm(r):
            layernorm("q", r, x1, x2n, st2, mv2, ve2, rstd2, [("x1_1", r)], [("q_tr1", r - 1)])

        def post_transpose(r, k):
            bank_free = [("x1_1", r)] if k == 0 else [("q_trc0", r)]
            transposed("q", k, r, x2n, x2T, PB, [("h_mm", r - 1), ("x2_out", r - 1)], bank_free)

        def post_route(r):
            op("S", lambda e, b: e.dma_start(x2_dram[chunk(b, r)], x2T[:, :, :]),
               after=[("q_trc1", r)], done=("q2", "x2_out"), r=r, carrier=True)
            for t in range(TB):
                for k in range(KD):
                    op("T", lambda e, b, t=t, k=k: e.matmul(
                        PB[:, t * NE:(t + 1) * NE], x2T[:, k, t * P:(t + 1) * P], w_r[:, k, :],
                        start=(k == 0), stop=(k == KD - 1)),
                       after=[("q_trc1", r)] if t == 0 and k == 0 else (),
                       done=("qt", "lg_mm") if t == TB - 1 and k == KD - 1 else None, r=r)
            op("V", lambda e, b: e.tensor_copy(lg[:, :, :], PB[:, 0:TB * NE].rearrange("p (t n) -> p t n", t=TB)),
               after=[("lg_mm", r), ("prob", r - 1)], done=("qv", "lg"), r=r)
            for t in range(TB):
                op("V", lambda e, b, t=t: e.max(top8[:, t, :], lg[:, t, :]),
                   after=[("lg", r)] if t == 0 else (), done=("qv", f"top{t}"), r=r, carrier=True)
            op("V", lambda e, b: e.tensor_tensor(gap[:, :], top8[:, :, 1], top8[:, :, 0], ALU.subtract),
               after=[(f"top{TB - 1}", r)], done=("qv", "gap"), r=r)
            op("A", lambda e, b: e.activation(gap[:, :], gap[:, :], ACT.Exp),
               after=[("gap", r)], done=("qa", "gap_e"), r=r)
            op("V", lambda e, b: e.tensor_scalar(p_top[:, :], gap[:, :], 1.0, None, ALU.add),
               after=[("gap_e", r)], done=("qv", "p_den"), r=r)
            op("V", lambda e, b: e.reciprocal(p_top[:, :], p_top[:, :]),
               after=[("p_den", r)], done=("qv", "p_top"), r=r)
            op("V", lambda e, b: e.tensor_scalar(p_top[:, :], p_top[:, :], 1.0, None, ALU.is_ge),
               after=[("p_top", r)], done=("qv", "p_tr"), r=r)
            op("V", lambda e, b: e.tensor_tensor(
                is_top[:, :, :], lg[:, :, :], top8[:, :, 0:1].broadcast_to([P, TB, NE]), ALU.is_ge),
               done=("qv", "is_top"), r=r)
            op("V", lambda e, b: e.tensor_tensor(
                prob[:, chunk(b, r), :, :] if isinstance(b, int) else
                prob[:, bass.ds(chunk(b, r), 1), :, :].rearrange("p o t n -> p (o t) n"),
                is_top[:, :, :], p_top[:, :].rearrange("p (t o) -> p t o", o=1).broadcast_to([P, TB, NE]), ALU.mult),
               after=[("is_top", r)], done=("qv", "prob"), r=r)

        def post_hidden(r):
            for k in range(KD):
                op("T", lambda e, b, k=k: e.matmul(PB[:, :], w_s1[:, k, :], x2T[:, k, :],
                                                   start=(k == 0), stop=(k == KD - 1)),
                   after=[("lg", r)] if k == 0 else (),
                   done=("qt", "h_mm") if k == KD - 1 else None, r=r)
            op("A", lambda e, b: e.activation(hT[:, :], PB[:, :], ACT.Relu),
               after=[("h_mm", r), ("o1_mm", r - 1)], done=("qa", "hr"), r=r)
            op("A", lambda e, b: e.activation(hT[:, :], hT[:, :], ACT.Square),
               after=[("hr", r)], done=("qa", "h"), r=r)

        def post_shared(r, k):
            for t2 in range(2):
                t = 2 * k + t2
                op("T", lambda e, b, t=t, t2=t2: e.matmul(
                    PB[:, t2 * DM:(t2 + 1) * DM], hT[:, t * P:(t + 1) * P], w_s2[:, :], start=True, stop=True),
                   after=[("o0" if k else "h", r)] if t2 == 0 else (),
                   done=("qt", f"o{k}_mm") if t2 else None, r=r)
            op("V", lambda e, b: e.tensor_tensor(
                x1[:, 2 * k:2 * k + 2, :], x1[:, 2 * k:2 * k + 2, :],
                PB[:, :].rearrange("p (t d) -> p t d", t=2), ALU.add),
               after=[(f"o{k}_mm", r)], done=("qv", f"o{k}"), r=r)

        def post_store(r):
            op("S", lambda e, b: e.dma_start(out_v[chunk(b, r)], x1[:, :, :]),
               after=[("o1", r)], done=("qo", "o"), r=r, carrier=True)

        pq = sb("pq", [P, TB, NE])
        s_f = sem("s_f")
        s_rw = sem("s_rw")
        halo0 = sb("halo0", [P, G, K - 1])

        def side(s, r, prep, post):
            if post:
                m = r - 1
                if s == 0:
                    post_load(m)
                if s == 1:
                    post_gate(m, 1)
                if s in (3, 4):
                    post_out(m, s - 3)
                if s == 5:
                    post_norm(m)
                if s in (7, 8):
                    post_transpose(m, s - 7)
                if s == 9:
                    post_route(m)
                    post_hidden(m)
                if s in (10, 11):
                    post_shared(m, s - 10)
                if s == 12:
                    post_store(m)
            if prep:
                m = r + 1
                if s == 0:
                    prep_load(m)
                if s == 2:
                    prep_norm(m)
                    prep_halo(m)
                if s in (4, 5):
                    prep_transpose(m, s - 4)
                if 6 <= s < 10:
                    prep_in(m, s - 6)
                if 10 <= s < 14:
                    prep_z(m, s - 10)
                if 14 <= s < 18:
                    prep_conv(m, s - 14)
                if s == 18:
                    prep_silu(m)
                if s == 19:
                    prep_x(m)
                if 20 <= s < 24:
                    prep_dt(m, s - 20)
                if s == 24:
                    prep_softplus(m)
                if s >= 25 and s - 25 < N // 4:
                    prep_cb(m, s - 25)
            if s == N + 1:
                post_gate(r, 0)

        def half(r, prep, post):
            for s in range(STEPS):
                nxt = (s + 1, r) if s + 1 < STEPS else (0, r + 1)
                if s + 1 < STEPS or prep:
                    main_bcast(*nxt)
                main_exp(s, r)
                main_scan(s, r)
                main_times_c(s, r)
                if s or post:
                    main_sum(*before(s, r, 1))
                side(s, r, prep, post)

        def prologue():
            prep_load(0)
            prep_norm(0)
            prep_halo(0)
            for k in range(KD):
                prep_transpose(0, k)
            for f in (prep_in, prep_z, prep_conv):
                for g in range(G):
                    f(0, g)
            prep_silu(0)
            prep_x(0)
            for g in range(G):
                prep_dt(0, g)
            prep_softplus(0)
            for j in range(N // 4):
                prep_cb(0, j)
            main_bcast(0, 0)

        def epilogue():
            m = HV - 1
            main_sum(STEPS - 1, m)
            post_load(m)
            post_gate(m, 1)
            for k in range(2):
                post_out(m, k)
            post_norm(m)
            for k in range(KD):
                post_transpose(m, k)
            post_route(m)
            post_hidden(m)
            for k in range(2):
                post_shared(m, k)
            post_store(m)

        wr1 = cb[:, :, :].rearrange("p n t -> p (n t)")[:, 0:NE * KD * F].rearrange(
            "p (e k f) -> p e k f", e=NE, k=KD)
        wr2 = cb[:, :, :].rearrange("p n t -> p (n t)")[:, NE * KD * F:NE * KD * F + NE * DM].rearrange(
            "p (e d) -> p e d", e=NE)
        PREV = -HV

        def routed():
            op("V", lambda e, b: e.tensor_copy(pq[:, :, :], prob[:, b, :, :] if isinstance(b, int) else
                                               prob[:, bass.ds(b, 1), :, :].rearrange("p o t n -> p (o t) n")),
               after=[(f"r_acc{NE - 1}_{TB - 1}", PREV)], done=("rv", "r_pq"))
            op("S", lambda e, b: e.dma_start(xnT[:, :, :], x2_dram[b]),
               after=[(f"r_h{NE - 1}_mm", PREV)], done=("ri", "r_x"), carrier=True)
            op("S", lambda e, b: e.dma_start(x1[:, :, :], out_v[b]),
               after=[("r_o", PREV)], done=("ra", "r_acc"), carrier=True)
            for x_ in range(NE):
                prev = (f"r_s{x_ - 1}", 0) if x_ else (f"r_s{NE - 1}", PREV)
                for k in range(KD):
                    op("T", lambda e, b, k=k, x_=x_: e.matmul(PA[:, :], wr1[:, x_, k, :], xnT[:, k, :],
                                                              start=(k == 0), stop=(k == KD - 1)),
                       after=[("r_x", 0), prev] if k == 0 else (),
                       done=("rt", f"r_h{x_}_mm") if k == KD - 1 else None)
                op("A", lambda e, b: e.activation(hT[:, :], PA[:, :], ACT.Relu),
                   after=[(f"r_h{x_}_mm", 0), (f"r_y{x_ - 1}_mm1", 0) if x_ else (f"r_y{NE - 1}_mm1", PREV)],
                   done=("rs", f"r_r{x_}"))
                op("A", lambda e, b: e.activation(hT[:, :], hT[:, :], ACT.Square),
                   after=[(f"r_r{x_}", 0)], done=("rs", f"r_s{x_}"))
                for k in range(2):
                    for t2 in range(2):
                        t = 2 * k + t2
                        op("T", lambda e, b, t=t, t2=t2, k=k, x_=x_: e.matmul(
                            Y[k][:, t2 * DM:(t2 + 1) * DM], hT[:, t * P:(t + 1) * P], wr2[:, x_, :],
                            start=True, stop=True),
                           after=[(f"r_s{x_}", 0), (f"r_acc{x_ - 1}_{2 * k + 1}", 0) if x_ else
                                  (f"r_acc{NE - 1}_{2 * k + 1}", PREV)] if t2 == 0 else (),
                           done=("rt", f"r_y{x_}_mm{k}") if t2 else None)
                for t in range(TB):
                    op("V", lambda e, b, t=t, x_=x_: e.scalar_tensor_tensor(
                        out=x1[:, t, :], in0=Y[t // 2][:, (t % 2) * DM:(t % 2 + 1) * DM],
                        scalar=pq[:, t, x_:x_ + 1], in1=x1[:, t, :], op0=ALU.mult, op1=ALU.add),
                       after=([("r_pq", 0), ("r_acc", 0)] if x_ == 0 and t == 0 else []) +
                       [(f"r_y{x_}_mm{t // 2}", 0)] + ([(f"r_acc{x_ - 1}_{t}", 0)] if x_ else []),
                       done=("rv", f"r_acc{x_}_{t}"))
            op("S", lambda e, b: e.dma_start(out_v[b], x1[:, :, :]),
               after=[(f"r_acc{NE - 1}_{TB - 1}", 0)], done=("ro", "r_o"), carrier=True)

        first, middle, last = {}, {}, {}
        q = first
        prologue()
        half(0, True, False)
        half(1, True, True)
        q = middle
        half(0, True, True)
        half(1, True, True)
        q = last
        half(0, True, True)
        half(1, False, True)
        epilogue()

        routed_q = {}
        q = routed_q
        routed()

        def run_routed(e, name):
            e.wait_ge(s_f, 3)
            some = e.value_load(flag[0:1, 0:1], min_val=0, max_val=1)
            with e.If(some > 0):
                if name == "S":
                    e.wait_ge(T["qo"].sem, 16 * NQ)
                    e.wait_ge(T["q2"].sem, 16 * NQ)
                    e.wait_ge(T["hc"].sem, STEPS * NQ)
                    e.dma_start(wr1, W1.rearrange("e (k p) f -> p e k f", p=P)).then_inc(s_rw, 16)
                    e.dma_start(wr2, W2.rearrange("e f d -> f e d")).then_inc(s_rw, 16)
                if name == "T":
                    e.wait_ge(s_rw, 32)
                for f in routed_q.get(name, ()):
                    f(e, 0)
                with e.Fori(1, NQ) as c:
                    for f in routed_q.get(name, ()):
                        f(e, c)
                if name == "S":
                    e.wait_ge(T["ro"].sem, 16 * NQ)

        def run(e, name):
            for f in first.get(name, ()):
                f(e, 0)
            with e.Fori(1, NB - 1) as b:
                for f in middle.get(name, ()):
                    f(e, b)
            for f in last.get(name, ()):
                f(e, NB - 1)

        block = ctx.enter_context(nc.Block())
        loads = [
            (w_in[:, :, :], in_wT.rearrange("(k p) e -> p k e", p=P)),
            (w_conv[:, :, :], conv_w.rearrange("(g p) o k -> p g (o k)", p=P)),
            (w_x[:, :, :], x_wT.rearrange("(g p) f -> p g f", p=P)),
            (w_dt[0:R, :], dt_wT),
            (b_dt[:, :], dt_b.rearrange("(g p) -> p g", p=P)),
            (a_log[:, :, :], A_log.rearrange("(g p) n -> p g n", p=P)),
            (d_skip[:, :], D.rearrange("(g p) -> p g", p=P)),
            (w_out[:, :, :], out_wT.rearrange("(g p) d -> p g d", p=P)),
            (w_s1[:, :, :], Ws1.rearrange("(k p) f -> p k f", p=P)),
            (w_s2[:, :], Ws2),
            (w_r[:, :, :], Wr.rearrange("(k p) e -> p k e", p=P)),
        ]

        @block.sync
        def _(e):
            for dst, src in loads:
                e.dma_start(dst, src, allow_slow_non_contiguous=len(dst.shape) == 2).then_inc(s_w, 16)
            run(e, "S")
            run_routed(e, "S")
            e.wait_ge(T["qo"].sem, 16 * NQ)
            e.wait_ge(T["q2"].sem, 16 * NQ)

        @block.gpsimd
        def _(e):
            e.memset(ident[:, :], 0.0).then_inc(s_g, 1)
            e.memset(sel[:, :, :], 0.0).then_inc(s_g, 1)
            e.memset(halo0[:, :, :], 0.0).then_inc(s_g, 1)
            e.memset(mhalf[:, :], -0.5).then_inc(s_g, 1)
            e.wait_ge(s_g, 4)
            e.affine_select(out=ident[:, :], in_=ident[:, :], compare_op=ALU.not_equal, fill=1.0, base=0,
                            pattern=[[-1, P]], channel_multiplier=1).then_inc(s_g, 1)
            for j in range(3):
                if j:
                    e.wait_ge(s_g, 5 + j)
                e.affine_select(out=sel[:, :, :], in_=sel[:, :, :], compare_op=ALU.not_equal, fill=1.0,
                                base=-32 * j, pattern=[[-1, N], [0, P]], channel_multiplier=1).then_inc(s_g, 1)
            e.wait_ge(s_g, 8)
            run(e, "G")

        @block.vector
        def _(e):
            e.wait_ge(s_g, 8)
            e.wait_ge(s_w, 16 * len(loads))
            e.memset(w_dt[R:FX, :], 0.0).then_inc(s_v0, 1)
            for g in range(G):
                for k in range(K):
                    e.tensor_scalar(w_diag[:, g, k, :], ident[:, :], w_conv[:, g, k:k + 1], None,
                                    ALU.mult).then_inc(s_v0, 1)
            e.wait_ge(s_a0, 1)
            e.tensor_scalar(a_neg[:, :, :], a_neg[:, :, :], -1.0, None, ALU.mult).then_inc(s_v0, 1)
            e.memset(ones[:, :], 1.0).then_inc(s_v0, 1)
            run(e, "V")
            last_prob = T["qv"].value(("prob", 1), NB - 1)
            e.wait_ge(T["qv"].sem, last_prob)
            e.tensor_reduce(any_p[:, :], prob[:, :, :, :].rearrange("p q t n -> p (q t n)"),
                            mybir.AxisListType.X, ALU.max).then_inc(s_f, 1)
            e.wait_ge(s_f, 2)
            e.tensor_scalar(flag[:, :], PA[0:1, 0:1], 1.0, None, ALU.min).then_inc(s_f, 1)
            run_routed(e, "V")

        @block.scalar
        def _(e):
            e.wait_ge(s_g, 8)
            e.wait_ge(s_w, 16 * len(loads))
            e.activation(a_neg[:, :, :], a_log[:, :, :], ACT.Exp).then_inc(s_a0, 1)
            e.wait_ge(s_v0, G * K + 2)
            run(e, "A")
            run_routed(e, "A")

        @block.tensor
        def _(e):
            e.wait_ge(s_g, 8)
            e.wait_ge(s_w, 16 * len(loads))
            e.wait_ge(s_v0, G * K + 1)
            run(e, "T")
            e.wait_ge(s_f, 1)
            e.matmul(PA[0:1, 0:1], any_p[:, :], ones[:, :], start=True, stop=True).then_inc(s_f, 1)
            run_routed(e, "T")


_INS = [("x", "L0_attn_x", None), ("in_wT", "L0_attn_in_proj_w", (1, 0)), ("conv_w", "L0_attn_conv_w", None),
        ("x_wT", "L0_attn_x_proj_w", (1, 0)), ("dt_wT", "L0_attn_dt_proj_w", (1, 0)),
        ("dt_b", "L0_attn_dt_proj_b", None), ("A_log", "L0_attn_A_log", None), ("D", "L0_attn_D", None),
        ("out_wT", "L0_attn_out_proj_w", (1, 0)), ("Ws1", "L0_ffn_Ws1", None), ("Ws2", "L0_ffn_Ws2", None),
        ("W1", "L0_ffn_W1", None), ("W2", "L0_ffn_W2", None), ("Wr", "L0_ffn_Wr", None)]


def kernel(**inputs):
    import numpy as _np
    import concourse.bacc as _bacc
    from concourse import mybir as _mybir
    from concourse.bass_utils import run_bass_kernel_spmd as _run

    nc = _bacc.Bacc("TRN2", target_bir_lowering=False, num_devices=1)
    arrays, args = {}, {}
    for name, source, order in _INS:
        a = _np.asarray(inputs[source])
        a = _np.ascontiguousarray(a if order is None else a.transpose(order))
        arrays[f"in_{name}"] = a
        args[name] = nc.dram_tensor(f"in_{name}", a.shape, _mybir.dt.from_np(a.dtype), kind="ExternalInput").ap()
    shape = inputs["L0_attn_x"].shape
    out = nc.dram_tensor("out_0", tuple(shape), _mybir.dt.float32, kind="ExternalOutput").ap()
    mamba_moe(nc, out=out, **args)
    r = _run(nc, [arrays], core_ids=[0])
    return r.results[0]["out_0"]
```

```python
from contextlib import ExitStack

import concourse.bass as bass
from concourse import mybir

F32 = mybir.dt.float32
BF16 = mybir.dt.bfloat16
I32 = mybir.dt.int32
ALU = mybir.AluOpType
ACT = mybir.ActivationFunctionType

P = 128
CH = 512
EPS = 1e-5
HC = 4
LAG = 2


class Track:

    def __init__(self, sem, amount=1):
        self.sem, self.amount, self.names, self.at = sem, amount, {}, 0
        self.closed = False

    def mark(self, name):
        if name in self.names:
            if self.names[name] == 1:
                self.closed = True
                self.at = 0
            assert self.names[name] == self.at + 1, (name, self.names[name], self.at)
        else:
            assert not self.closed, name
            self.names[name] = self.at + 1
        self.at += 1

    def value(self, name, seq):
        if isinstance(seq, int) and seq < 0:
            return None
        return (seq * len(self.names) + self.names[name]) * self.amount


def mamba_moe(nc, x, in_wT, conv_w, x_wT, dt_wT, dt_b, A_log, D, out_wT, Ws1, Ws2, W1, W2, Wr, out):
    NB, L, DM = x.shape
    ED = out_wT.shape[0]
    N = A_log.shape[1]
    K = conv_w.shape[2]
    R = dt_wT.shape[0]
    F = Ws1.shape[1]
    NE = Wr.shape[1]
    G = ED // P
    KD = DM // P
    TB = CH // P
    HV = L // CH
    NQ = NB * HV
    FX = R + 2 * N
    NG2 = G // 2
    STEPS = NG2 * N
    assert HV == 2 and KD == 2 and FX == 96 and N == 16 and F == P

    x_v = x.rearrange("b (h t p) d -> (b h) p t d", h=HV, p=P)
    out_v = out.rearrange("b (h t p) d -> (b h) p t d", h=HV, p=P)
    c_dram = nc.dram_tensor("c_scratch", (HV, N, CH), F32, kind="Internal").ap()
    x2_dram = nc.dram_tensor("x2_scratch", (NQ, P, KD, CH), F32, kind="Internal").ap()

    with ExitStack() as ctx:
        def sb(name, shape, dt=F32):
            return ctx.enter_context(nc.sbuf_tensor(name, shape, dt))

        def pb(name):
            return ctx.enter_context(nc.psum_tensor(name, [P, 512], F32))

        def sem(name):
            return ctx.enter_context(nc.semaphore(name))

        w_in = sb("w_in", [P, KD, 2 * ED])
        w_conv = sb("w_conv", [P, G, K])
        w_diag = sb("w_diag", [P, G, K, P])
        d_diag = sb("d_diag", [P, G, P])
        w_x = sb("w_x", [P, G, FX])
        w_dt = sb("w_dt", [FX, ED])
        b_dt = sb("b_dt", [P, G])
        a_log = sb("a_log", [P, G, N])
        a_neg = sb("a_neg", [P, G, N])
        d_skip = sb("d_skip", [P, G])
        w_out = sb("w_out", [P, G, DM])
        w_s1 = sb("w_s1", [P, KD, F])
        w_s2 = sb("w_s2", [P, DM])
        w_r = sb("w_r", [P, KD, NE])
        ident = sb("ident", [P, P])
        sel = sb("sel", [FX, N, P], BF16)
        mhalf = sb("mhalf", [P, TB])
        xt = sb("xt", [P, TB, DM])
        st = sb("st", [P, TB, 6])
        mv = sb("mv", [P, TB, 2])
        ve = sb("ve", [P, TB])
        rstd = sb("rstd", [P, TB])
        xnT = sb("xnT", [P, KD, CH])
        xp = sb("xp", [P, G, K - 1 + CH])
        xc = [sb(f"xc{h}", [P, G, CH]) for h in range(HV)]
        gate = [sb(f"gate{h}", [P, TB, ED]) for h in range(HV)]
        delta = [sb(f"delta{h}", [P, G, CH]) for h in range(HV)]
        u = [sb(f"u{h}", [P, G, CH]) for h in range(HV)]
        dbc = sb("dbc", [FX, CH])
        xt_flat = xt[:, :, :].rearrange("p t d -> p (t d)")
        bc_r = xt_flat[0:FX, 0:CH]
        bc_hi = xt_flat[0:FX, CH:CH + CH // 2].bitcast(BF16)
        bc_mid = xt_flat[0:FX, CH + CH // 2:2 * CH].bitcast(BF16)
        bc3 = [sb(f"bc3_{h}", [FX, CH], BF16) for h in range(HV)]
        cb = sb("cb", [P, N, CH])
        bx = [sb(f"bx{i}", [P, 2, CH]) for i in range(2)]
        hs = [sb(f"hs{i}", [P, 2, CH]) for i in range(2)]
        hc = [sb(f"hc{i}", [P, 2, CH]) for i in range(HC)]
        hlast = sb("hlast", [P, STEPS, 2])
        ygT = sb("ygT", [P, G, CH])
        x1 = sb("x1", [P, TB, DM])
        x2n = sb("x2n", [P, TB, DM])
        st2 = sb("st2", [P, TB, 6])
        mv2 = sb("mv2", [P, TB, 2])
        ve2 = sb("ve2", [P, TB])
        rstd2 = sb("rstd2", [P, TB])
        x2T = sb("x2T", [P, KD, CH])
        hT = sb("hT", [P, CH])
        lg = sb("lg", [P, TB, NE])
        top8 = sb("top8", [P, TB, 8])
        gap = sb("gap", [P, TB])
        p_top = sb("p_top", [P, TB])
        is_top = sb("is_top", [P, TB, NE])
        prob = sb("prob", [P, NQ, TB, NE])
        any_p = sb("any_p", [P, 1])
        ones = sb("ones", [P, 1])
        flag = sb("flag", [1, 1], I32)
        Y = [pb("Y0"), pb("Y1")]
        BB = [pb("BB0"), pb("BB1")]
        DA = [pb("DA0"), pb("DA1")]
        PA, PB = pb("PA"), pb("PB")

        s_w = sem("s_w")
        s_g = sem("s_g")
        s_v0 = sem("s_v0")
        s_a0 = sem("s_a0")
        T = {
            "bb": Track(sem("m_bb")), "da": Track(sem("m_da")), "bx": Track(sem("m_bx")),
            "sc": Track(sem("m_sc")), "hl": Track(sem("m_hl")), "hc": Track(sem("m_hc")),
            "y": Track(sem("m_y")), "y0": Track(sem("m_y0")), "yg": Track(sem("m_yg")),
            "px": Track(sem("p_x"), 16), "pt": Track(sem("p_t")), "pv": Track(sem("p_v")),
            "pa": Track(sem("p_a")), "pg": Track(sem("p_g")),
            "pc": Track(sem("p_c"), 16), "cb": Track(sem("p_cb"), 16),
            "qx": Track(sem("q_x"), 16), "qt": Track(sem("q_t")), "qv": Track(sem("q_v")),
            "qa": Track(sem("q_a")), "qg": Track(sem("q_g")), "qo": Track(sem("q_o"), 16),
            "q2": Track(sem("q_x2"), 16),
            "ri": Track(sem("r_in"), 16), "ra": Track(sem("r_acc"), 16), "ro": Track(sem("r_out"), 16),
            "rt": Track(sem("r_t")), "rs": Track(sem("r_a")), "rv": Track(sem("r_v")),
        }
        where = {}

        queues = {}
        q = None

        s_carry = {"V": sem("carry_v"), "G": sem("carry_g"), "S": sem("carry_s")}

        def op(engine, make, after=(), done=None, r=0, carrier=False):
            if done:
                T[done[0]].mark((done[1], r % HV))
                where[done[1]] = T[done[0]]

            def run(e, b):
                for name, c in after:
                    track = where[name]
                    v = track.value((name, c % HV), b + c // HV)
                    if v is not None:
                        e.wait_ge(track.sem, v)
                        if engine == "S" and not isinstance(v, int):
                            e.sem_inc(s_carry[engine], 1)
                if carrier and engine != "S" and after and not isinstance(b, int):
                    e.sem_inc(s_carry[engine], 1)
                ins = make(e, b)
                if done:
                    ins.then_inc(T[done[0]].sem, T[done[0]].amount)
            q.setdefault(engine, []).append(run)

        def chunk(b, r):
            return b * HV + r

        def norm_stats(pre, r, src, stt, mvt, vet, rt, ready):
            tv, tg = pre + "v", pre + "g"
            for t in range(TB):
                op("V", lambda e, b, t=t: e.bn_stats(stt[:, t, :], src[:, t, :]),
                   after=ready if t == 0 else (), done=(tv, f"{pre}_st{t}"), r=r)
            for t in range(TB):
                w = [(f"{pre}_st{t}", r)]
                if t == 0:
                    w.append((f"{pre}_ve", r - 1))
                op("V", lambda e, b, t=t: e.bn_aggr(mvt[:, t, :], stt[:, t, :]),
                   after=w, done=(tv, f"{pre}_mv{t}"), r=r, carrier=True)
            op("G", lambda e, b: e.tensor_scalar(vet[:, :], mvt[:, :, 1], EPS, None, ALU.add),
               after=[(f"{pre}_mv{TB - 1}", r), (f"{pre}_rstd", r - 1)], done=(tg, f"{pre}_ve"), r=r, carrier=True)
            op("G", lambda e, b: e.tensor_tensor(rt[:, :], vet[:, :], mhalf[:, :], ALU.pow),
               after=[(f"{pre}_ve", r), (f"{pre}_n{TB - 1}", r - 1)], done=(tg, f"{pre}_rstd"), r=r)

        def norm_apply(pre, r, src, dst, mvt, rt, freed):
            tv = pre + "v"
            for t in range(TB):
                op("V", lambda e, b, t=t: e.tensor_scalar(
                    dst[:, t, :], src[:, t, :], mvt[:, t, 0:1], rt[:, t:t + 1], ALU.subtract, ALU.mult),
                   after=([(f"{pre}_rstd", r)] + freed) if t == 0 else (), done=(tv, f"{pre}_n{t}"), r=r)

        def transposed(pre, k, r, src, dst, bank, freed, bank_free):
            for t in range(TB):
                op("T", lambda e, b, t=t: e.transpose(
                    bank[:, t * P:(t + 1) * P], src[:, t, k * P:(k + 1) * P], ident[:, :]),
                   after=[(f"{pre}_n{t}", r)] + (bank_free if t == 0 else []),
                   done=(pre + "t", f"{pre}_tr{k}") if t == TB - 1 else None, r=r)
            op("A", lambda e, b: e.activation(dst[:, k, :], bank[:, :], ACT.Copy),
               after=[(f"{pre}_tr{k}", r)] + freed, done=(pre + "a", f"{pre}_trc{k}"), r=r)

        def prep_load(r):
            op("S", lambda e, b: e.dma_start(xt[:, :, :], x_v[chunk(b, r)]),
               after=[("b_lo", r - 1), ("b_mid0", r - 1)], done=("px", "x"), r=r, carrier=True)

        def prep_stats(r):
            norm_stats("p", r, xt, st, mv, ve, rstd, [("x", r)])

        def prep_norm(r):
            norm_apply("p", r, xt, xt, mv, rstd, [])

        def prep_transpose(r, k):
            bank_free = [("sp3", r - 1)] if k == 0 else [("p_trc0", r)]
            transposed("p", k, r, xt, xnT, PA, [("z3_mm", r - 1)], bank_free)

        def prep_halo(r):
            halo = xp[:, :, 0:K - 1]
            if r % HV == 0:
                op("A", lambda e, b: e.activation(
                    halo, halo0[:, :, :], ACT.Copy),
                   after=[("cv3_mm", r - 1), ("halo", r - 1)], done=("pa", "halo"), r=r)
            else:
                op("A", lambda e, b: e.activation(halo, xp[:, :, CH:CH + K - 1], ACT.Copy),
                   after=[("cv3_mm", r - 1), ("xp3", r - 1)], done=("pa", "halo"), r=r)

        def prep_in(r, g):
            for k in range(KD):
                op("T", lambda e, b, k=k: e.matmul(PA[:, :], w_in[:, k, g * P:(g + 1) * P], xnT[:, k, :],
                                                   start=(k == 0), stop=(k == KD - 1)),
                   after=[("p_trc1" if g == 0 else f"xp{g - 1}", r)] if k == 0 else (),
                   done=("pt", f"xp{g}_mm") if k == KD - 1 else None, r=r)
            op("A", lambda e, b: e.activation(xp[:, g, K - 1:], PA[:, :], ACT.Copy),
               after=[(f"xp{g}_mm", r), ("halo", r)], done=("pa", f"xp{g}"), r=r)

        def prep_z(r, t):
            for k in range(KD):
                op("T", lambda e, b, k=k: e.matmul(
                    PA[:, :], xnT[:, k, t * P:(t + 1) * P], w_in[:, k, ED:2 * ED],
                    start=(k == 0), stop=(k == KD - 1)),
                   after=[("xp3" if t == 0 else f"z{t - 1}", r)] if k == 0 else (),
                   done=("pt", f"z{t}_mm") if k == KD - 1 else None, r=r)
            op("A", lambda e, b: e.activation(gate[r % HV][:, t, :], PA[:, :], ACT.Copy),
               after=[(f"z{t}_mm", r), ("yt3_mm", r - 2)], done=("pa", f"z{t}"), r=r)

        def prep_conv(r, g, part):
            for k in range(part * K // 2, (part + 1) * K // 2):
                op("T", lambda e, b, k=k: e.matmul(PA[:, :], w_diag[:, g, k, :], xp[:, g, k:k + CH],
                                                   start=(k == 0), stop=(k == K - 1)),
                   after=[("z3" if g == 0 else f"cv{g - 1}", r)] if k == 0 else (),
                   done=("pt", f"cv{g}_mm") if k == K - 1 else None, r=r)
            if part:
                op("A", lambda e, b: e.activation(xc[r % HV][:, g, :], PA[:, :], ACT.Copy),
                   after=[(f"cv{g}_mm", r), ("dx1", r - 2)], done=("pa", f"cv{g}"), r=r)

        def prep_silu(r):
            h = r % HV
            op("A", lambda e, b: e.activation(xc[h][:, :, :], xc[h][:, :, :], ACT.Silu),
               after=[("cv3", r)], done=("pa", "xc"), r=r)
            op("A", lambda e, b: e.activation(gate[h][:, :, :], gate[h][:, :, :], ACT.Silu),
               after=[("z3", r)], done=("pa", "gate"), r=r)

        def prep_x_mm(r, part):
            h = r % HV
            for g in range(part * G // 2, (part + 1) * G // 2):
                op("T", lambda e, b, g=g: e.matmul(PA[0:FX, :], w_x[:, g, :], xc[h][:, g, :],
                                                   start=(g == 0), stop=(g == G - 1)),
                   after=[("xc", r)] if g == 0 else (),
                   done=("pt", "xw_mm") if g == G - 1 else None, r=r)

        def prep_x(r):
            h = r % HV
            lo, hi = FX - 2 * N, FX
            op("A", lambda e, b: e.activation(dbc[:, :], PA[0:FX, :], ACT.Copy),
               after=[("xw_mm", r), ("dt3_mm", r - 1), ("b_r", r - 1), ("c_out", r - 1)],
               done=("pa", "dbc"), r=r)
            op("S", lambda e, b: e.dma_start(c_dram[h], dbc[R + N:FX, :]),
               after=[("dbc", r), (f"cb{N // 4 - 1}", r - 2)], done=("pc", "c_out"), r=r)
            op("A", lambda e, b: e.activation(bc_hi[lo:hi, :], dbc[lo:hi, :], ACT.Copy),
               after=[("dbc", r), ("p_tr1", r)], done=("pa", "b_hi"), r=r)
            op("A", lambda e, b: e.activation(bc3[h][0:32, :], dbc[lo:hi, :], ACT.Copy),
               after=[(f"bb{STEPS - 1}", r - 2)], done=("pa", "b_hi0"), r=r)
            op("V", lambda e, b: e.tensor_tensor(bc_r[lo:hi, :], dbc[lo:hi, :], bc_hi[lo:hi, :], ALU.subtract),
               after=[("b_hi", r), ("b_mid0", r - 1)], done=("pv", "b_r"), r=r)
            op("A", lambda e, b: e.activation(bc_mid[lo:hi, :], bc_r[lo:hi, :], ACT.Copy),
               after=[("b_r", r)], done=("pa", "b_mid"), r=r)
            op("A", lambda e, b: e.activation(bc3[h][32:64, :], bc_r[lo:hi, :], ACT.Copy),
               after=(), done=("pa", "b_mid0"), r=r)
            op("V", lambda e, b: e.tensor_tensor(bc3[h][lo:hi, :], bc_r[lo:hi, :], bc_mid[lo:hi, :], ALU.subtract),
               after=[("b_mid", r), (f"bb{STEPS - 1}", r - 2)], done=("pv", "b_lo"), r=r)

        def prep_dt(r, g):
            h = r % HV
            op("T", lambda e, b: e.matmul(PA[:, :], w_dt[:, g * P:(g + 1) * P], dbc[:, :], start=True, stop=True),
               after=[("dbc" if g == 0 else f"sp{g - 1}", r)], done=("pt", f"dt{g}_mm"), r=r)
            op("A", lambda e, b: e.activation(delta[h][:, g, :], PA[:, :], ACT.Identity, bias=b_dt[:, g:g + 1]),
               after=[(f"dt{g}_mm", r), (f"da{STEPS - 1}_1", r - 2), ("u1", r - 2)], done=("pa", f"dt{g}"), r=r)
            op("A", lambda e, b: e.activation(u[h][:, g, :], PA[:, :], ACT.Abs, bias=b_dt[:, g:g + 1]),
               after=[(f"bx{STEPS - 1}", r - 2)], done=("pa", f"sp{g}"), r=r)

        def prep_softplus(r, pair, part):
            h = r % HV
            pr = slice(2 * pair, 2 * pair + 2)
            if part == 0:
                op("A", lambda e, b: e.activation(u[h][:, pr, :], u[h][:, pr, :], ACT.Exp, scale=-1.0),
                   after=[(f"sp{2 * pair + 1}", r)], done=("pa", f"se{pair}"), r=r)
            elif part == 1:
                op("A", lambda e, b: e.activation(u[h][:, pr, :], u[h][:, pr, :], ACT.Ln, bias=1.0),
                   after=[(f"se{pair}", r)], done=("pa", f"sl{pair}"), r=r)
            else:
                op("V", lambda e, b: e.scalar_tensor_tensor(
                    out=delta[h][:, pr, :], in0=delta[h][:, pr, :], scalar=0.0, in1=u[h][:, pr, :],
                    op0=ALU.max, op1=ALU.add),
                   after=[(f"sl{pair}", r)], done=("pv", f"delta{pair}"), r=r)
                op("V", lambda e, b: e.tensor_tensor(u[h][:, pr, :], delta[h][:, pr, :], xc[h][:, pr, :], ALU.mult),
                   after=[(f"delta{pair}", r), ("xc", r)], done=("pv", f"u{pair}"), r=r)

        def prep_cb(r, j):
            h = r % HV
            op("S", lambda e, b: e.dma_start(cb[:, 4 * j:4 * j + 4, :],
                                             c_dram[h, 4 * j:4 * j + 4, :].partition_broadcast(P)),
               after=[("c_out", r), (f"hc{STEPS - N + 4 * j + 3}", r - 1)]
               + ([(f"cb{j - 1}", r)] if j else [(f"cb{N // 4 - 1}", r - 1)]),
               done=("cb", f"cb{j}"), r=r)

        def before(s, r, d):
            s -= d
            return (s, r) if s >= 0 else (s + STEPS, r - 1)

        def after_step(name, s, r, d, tail=""):
            s, r = before(s, r, d)
            return (f"{name}{s}{tail}", r)

        def main_bcast(s, r):
            op("T", lambda e, b: e.matmul(BB[s % 2][:, :], sel[:, s % N, :], bc3[r % HV][:, :],
                                          start=True, stop=True),
               after=[after_step("bx", s, r, 2)] + ([("b_lo", r), ("b_mid0", r)] if s == 0 else []),
               done=("bb", f"bb{s}"), r=r)

        def main_exp(s, r):
            pair, n = divmod(s, N)
            for g in range(2):
                gg = 2 * pair + g
                op("A", lambda e, b, g=g, gg=gg: e.activation(
                    DA[g][:, :], delta[r % HV][:, gg, :], ACT.Exp, scale=a_neg[:, gg, n:n + 1]),
                   after=[after_step("sc", s, r, 1, f"_{g}")] + ([(f"delta{pair}", r)] if n == 0 else []),
                   done=("da", f"da{s}_{g}"), r=r)

        def main_bx(s, r):
            pair, n = divmod(s, N)
            h = r % HV
            op("V", lambda e, b: e.tensor_tensor(
                bx[s % 2][:, :, :], u[h][:, 2 * pair:2 * pair + 2, :],
                BB[s % 2][:, :].rearrange("p (o t) -> p o t", o=1).broadcast_to([P, 2, CH]), ALU.mult),
               after=[(f"bb{s}", r), after_step("sc", s, r, 2, "_1")] + ([(f"u{pair}", r)] if n == 0 else []),
               done=("bx", f"bx{s}"), r=r)

        def main_scan(s, r, g):
            h = r % HV
            first = 0.0 if h == 0 else hlast[:, s, g:g + 1]
            wait = [(f"da{s}_{g}", r)]
            if g == 0:
                wait += [(f"bx{s}", r), after_step("hc", s, r, 2)]
                if h:
                    wait.append((f"hl{s}", r - 1))
            op("V", lambda e, b: e.tensor_tensor_scan(
                hs[s % 2][:, g, :], DA[g][:, :], bx[s % 2][:, g, :], first, ALU.mult, ALU.add),
               after=wait, done=("sc", f"sc{s}_{g}"), r=r)

        def main_keep(s, r):
            if r % HV == 0:
                op("V", lambda e, b: e.tensor_copy(hlast[:, s, :], hs[s % 2][:, :, CH - 1]),
                   after=[(f"sc{s}_1", r)], done=("hl", f"hl{s}"), r=r)

        def main_times_c(s, r):
            n = s % N
            op("G", lambda e, b: e.tensor_tensor(
                hc[s % HC][:, :, :], hs[s % 2][:, :, :],
                cb[:, n:n + 1, :].broadcast_to([P, 2, CH]), ALU.mult),
               after=[(f"sc{s}_1", r)] + [after_step("y", s, r, HC)]
               + ([(f"cb{n // 4}", r)] if s < N and n % 4 == 0 else []),
               done=("hc", f"hc{s}"), r=r)

        def y_at(t, g):
            return Y[t // 2][:, (t % 2) * 2 * P + g * P:(t % 2) * 2 * P + (g + 1) * P]

        def main_start(pair, r):
            h = r % HV
            for t in range(TB):
                for g in range(2):
                    w = []
                    if t == 0 and g == 0:
                        w = [("yg0", r) if pair else ("yg1", r - 1), ("xc", r)]
                    op("T", lambda e, b, t=t, g=g: e.matmul(
                        y_at(t, g), xc[h][:, 2 * pair + g, t * P:(t + 1) * P], d_diag[:, 2 * pair + g, :],
                        start=(t % 2 == 0 and g == 0), stop=False, skip_group_check=True),
                       after=w, done=("y0", f"dx{pair}") if t == TB - 1 and g else None, r=r)

        def main_sum(s, r):
            n = s % N
            for t in range(TB):
                for g in range(2):
                    op("T", lambda e, b, t=t, g=g: e.matmul(
                        y_at(t, g), hc[s % HC][:, g, t * P:(t + 1) * P], ident[:, :], is_transpose=True,
                        start=False, stop=(n == N - 1), skip_group_check=True),
                       after=[(f"hc{s}", r)] if t == 0 and g == 0 else (),
                       done=("y", f"y{s}") if t == TB - 1 and g else None, r=r)

        def post_gate(r, pair):
            h = r % HV
            for k in range(2):
                part = gate[h][:, 2 * k:2 * k + 2, pair * 2 * P:(pair + 1) * 2 * P]
                op("V", lambda e, b, k=k, part=part: e.tensor_tensor(
                    part, part, Y[k][:, :].rearrange("p (t c) -> p t c", t=2), ALU.mult),
                   after=[(f"y{pair * N + N - 1}", r), ("gate", r)] if k == 0 else (),
                   done=("yg", f"yg{pair}" if k else f"yg{pair}_"), r=r)

        def post_back(r, g):
            h = r % HV
            for t in range(TB):
                op("T", lambda e, b, t=t: e.transpose(PB[:, t * P:(t + 1) * P], gate[h][:, t, g * P:(g + 1) * P],
                                                      ident[:, :]),
                   after=[("yg0", r), ("yg1", r), (f"yt{g - 1}", r) if g else ("o1", r - 1)] if t == 0 else (),
                   done=("qt", f"yt{g}_mm") if t == TB - 1 else None, r=r)
            op("A", lambda e, b: e.activation(ygT[:, g, :], PB[:, :], ACT.Copy),
               after=[(f"yt{g}_mm", r), ("op1_mm", r - 1)], done=("qa", f"yt{g}"), r=r)

        def post_load(r):
            op("S", lambda e, b: e.dma_start(x1[:, :, :], x_v[chunk(b, r)]),
               after=[("o", r - 1)], done=("qx", "xr"), r=r, carrier=True)

        def post_out(r, t):
            k, t2 = divmod(t, 2)
            for g in range(G):
                w = []
                if t2 == 0 and g == 0:
                    w = [("yt3", r)] + ([("x1_0", r)] if k else [])
                op("T", lambda e, b, g=g: e.matmul(
                    PB[:, t2 * DM:(t2 + 1) * DM], ygT[:, g, t * P:(t + 1) * P], w_out[:, g, :],
                    start=(g == 0), stop=(g == G - 1)),
                   after=w, done=("qt", f"op{k}_mm") if t2 == 1 and g == G - 1 else None, r=r)
            if t2:
                op("V", lambda e, b: e.tensor_tensor(
                    x1[:, 2 * k:2 * k + 2, :], x1[:, 2 * k:2 * k + 2, :],
                    PB[:, :].rearrange("p (t d) -> p t d", t=2), ALU.add),
                   after=[(f"op{k}_mm", r), ("xr", r)], done=("qv", f"x1_{k}"), r=r)

        def post_stats(r):
            norm_stats("q", r, x1, st2, mv2, ve2, rstd2, [("x1_1", r)])

        def post_norm(r):
            norm_apply("q", r, x1, x2n, mv2, rstd2, [("q_tr1", r - 1)])

        def post_transpose(r, k):
            bank_free = [("x1_1", r)] if k == 0 else [("q_trc0", r)]
            transposed("q", k, r, x2n, x2T, PB, [("h_mm", r - 1), ("x2_out", r - 1)], bank_free)

        def post_route(r):
            op("S", lambda e, b: e.dma_start(x2_dram[chunk(b, r)], x2T[:, :, :]),
               after=[("q_trc1", r)], done=("q2", "x2_out"), r=r, carrier=True)
            for t in range(TB):
                for k in range(KD):
                    op("T", lambda e, b, t=t, k=k: e.matmul(
                        PB[:, t * NE:(t + 1) * NE], x2T[:, k, t * P:(t + 1) * P], w_r[:, k, :],
                        start=(k == 0), stop=(k == KD - 1)),
                       after=[("q_trc1", r)] if t == 0 and k == 0 else (),
                       done=("qt", "lg_mm") if t == TB - 1 and k == KD - 1 else None, r=r)
            op("V", lambda e, b: e.tensor_copy(lg[:, :, :], PB[:, 0:TB * NE].rearrange("p (t n) -> p t n", t=TB)),
               after=[("lg_mm", r), ("prob", r - 1)], done=("qv", "lg"), r=r)
            for t in range(TB):
                op("V", lambda e, b, t=t: e.max(top8[:, t, :], lg[:, t, :]),
                   after=[("lg", r)] if t == 0 else (), done=("qv", f"top{t}"), r=r, carrier=True)
            op("V", lambda e, b: e.tensor_tensor(gap[:, :], top8[:, :, 1], top8[:, :, 0], ALU.subtract),
               after=[(f"top{TB - 1}", r)], done=("qv", "gap"), r=r)
            op("A", lambda e, b: e.activation(gap[:, :], gap[:, :], ACT.Exp),
               after=[("gap", r)], done=("qa", "gap_e"), r=r)
            op("V", lambda e, b: e.tensor_scalar(p_top[:, :], gap[:, :], 1.0, None, ALU.add),
               after=[("gap_e", r)], done=("qv", "p_den"), r=r)
            op("V", lambda e, b: e.reciprocal(p_top[:, :], p_top[:, :]),
               after=[("p_den", r)], done=("qv", "p_top"), r=r)
            op("V", lambda e, b: e.tensor_scalar(p_top[:, :], p_top[:, :], 1.0, None, ALU.is_ge),
               after=[("p_top", r)], done=("qv", "p_tr"), r=r)
            op("V", lambda e, b: e.tensor_tensor(
                is_top[:, :, :], lg[:, :, :], top8[:, :, 0:1].broadcast_to([P, TB, NE]), ALU.is_ge),
               done=("qv", "is_top"), r=r)
            op("V", lambda e, b: e.tensor_tensor(
                prob[:, chunk(b, r), :, :] if isinstance(b, int) else
                prob[:, bass.ds(chunk(b, r), 1), :, :].rearrange("p o t n -> p (o t) n"),
                is_top[:, :, :], p_top[:, :].rearrange("p (t o) -> p t o", o=1).broadcast_to([P, TB, NE]), ALU.mult),
               after=[("is_top", r)], done=("qv", "prob"), r=r)

        def post_hidden(r):
            for k in range(KD):
                op("T", lambda e, b, k=k: e.matmul(PB[:, :], w_s1[:, k, :], x2T[:, k, :],
                                                   start=(k == 0), stop=(k == KD - 1)),
                   after=[("lg", r)] if k == 0 else (),
                   done=("qt", "h_mm") if k == KD - 1 else None, r=r)
            op("A", lambda e, b: e.activation(hT[:, :], PB[:, :], ACT.Relu),
               after=[("h_mm", r), ("o1_mm", r - 1)], done=("qa", "hr"), r=r)
            op("A", lambda e, b: e.activation(hT[:, :], hT[:, :], ACT.Square),
               after=[("hr", r)], done=("qa", "h"), r=r)

        def post_shared(r, k):
            for t2 in range(2):
                t = 2 * k + t2
                op("T", lambda e, b, t=t, t2=t2: e.matmul(
                    PB[:, t2 * DM:(t2 + 1) * DM], hT[:, t * P:(t + 1) * P], w_s2[:, :], start=True, stop=True),
                   after=[("o0" if k else "h", r)] if t2 == 0 else (),
                   done=("qt", f"o{k}_mm") if t2 else None, r=r)
            op("V", lambda e, b: e.tensor_tensor(
                x1[:, 2 * k:2 * k + 2, :], x1[:, 2 * k:2 * k + 2, :],
                PB[:, :].rearrange("p (t d) -> p t d", t=2), ALU.add),
               after=[(f"o{k}_mm", r)], done=("qv", f"o{k}"), r=r)

        def post_store(r):
            op("S", lambda e, b: e.dma_start(out_v[chunk(b, r)], x1[:, :, :]),
               after=[("o1", r)], done=("qo", "o"), r=r, carrier=True)

        pq = sb("pq", [P, TB, NE])
        s_f = sem("s_f")
        s_rw = sem("s_rw")
        halo0 = sb("halo0", [P, G, K - 1])

        LOAD = [(26, prep_load)]
        PREP = [(0, prep_stats), (1, prep_norm), (1, prep_halo)]
        PREP += [(3 + k, prep_transpose, k) for k in range(KD)]
        PREP += [(5 + g, prep_in, g) for g in range(G)]
        PREP += [(9 + t, prep_z, t) for t in range(TB)]
        PREP += [(13 + 2 * g + p_, prep_conv, g, p_) for g in range(G) for p_ in range(2)]
        PREP += [(21, prep_silu), (22, prep_x_mm, 0), (23, prep_x_mm, 1), (23, prep_x)]
        PREP += [(24, prep_dt, 0), (25, prep_dt, 1), (26, prep_softplus, 0, 0), (26, prep_dt, 2),
                 (27, prep_softplus, 0, 1), (27, prep_dt, 3), (28, prep_softplus, 0, 2),
                 (28, prep_softplus, 1, 0), (29, prep_softplus, 1, 1), (30, prep_softplus, 1, 2)]
        PREP += [(24 + 2 * j, prep_cb, j) for j in range(N // 4)]
        POST = [(0, post_load), (2, post_gate, 1)]
        POST += [(3 + g // 2, post_back, g) for g in range(G)]
        POST += [(21, post_out, 0), (24, post_out, 1), (25, post_out, 2), (26, post_out, 3), (27, post_stats),
                 (28, post_norm), (29, post_transpose, 0), (29, post_transpose, 1), (30, post_route),
                 (30, post_hidden), (31, post_shared, 0), (31, post_shared, 1), (31, post_store)]

        def side(s, r, prep, post, load):
            for items, r2, wanted in ((POST, r - 1, post), (PREP, r + 1, prep), (LOAD, r + 2, load)):
                for at, f, *args in items:
                    if wanted and at == s:
                        f(r2, *args)
            if s == 2:
                main_start(0, r)
            if s == N + LAG:
                post_gate(r, 0)
                main_start(1, r)

        def half(r, prep, post, load):
            for s in range(STEPS):
                def step(d):
                    return (s + d, r) if s + d < STEPS else (s + d - STEPS, r + 1)

                if s + 2 < STEPS or prep:
                    main_bcast(*step(2))
                main_exp(s, r)
                main_scan(s, r, 0)
                if s or r % HV:
                    main_keep(*before(s, r, 1))
                if s + 1 < STEPS or prep:
                    main_bx(*step(1))
                main_scan(s, r, 1)
                main_times_c(s, r)
                if s < LAG:
                    if post:
                        main_sum(*before(s, r, LAG))
                    side(s, r, prep, post, load)
                else:
                    side(s, r, prep, post, load)
                    main_sum(s - LAG, r)

        def prologue():
            prep_load(0)
            for at, f, *args in sorted(PREP, key=lambda item: item[0]):
                f(0, *args)
            prep_load(1)
            main_bcast(0, 0)
            main_bcast(1, 0)
            main_bx(0, 0)

        def epilogue():
            m = HV - 1
            for s in range(STEPS - LAG, STEPS):
                main_sum(s, m)
            for at, f, *args in POST:
                f(m, *args)

        wr1 = cb[:, :, :].rearrange("p n t -> p (n t)")[:, 0:NE * KD * F].rearrange(
            "p (e k f) -> p e k f", e=NE, k=KD)
        wr2 = cb[:, :, :].rearrange("p n t -> p (n t)")[:, NE * KD * F:NE * KD * F + NE * DM].rearrange(
            "p (e d) -> p e d", e=NE)
        PREV = -HV

        def routed():
            op("V", lambda e, b: e.tensor_copy(pq[:, :, :], prob[:, b, :, :] if isinstance(b, int) else
                                               prob[:, bass.ds(b, 1), :, :].rearrange("p o t n -> p (o t) n")),
               after=[(f"r_acc{NE - 1}_{TB - 1}", PREV)], done=("rv", "r_pq"))
            op("S", lambda e, b: e.dma_start(xnT[:, :, :], x2_dram[b]),
               after=[(f"r_h{NE - 1}_mm", PREV)], done=("ri", "r_x"), carrier=True)
            op("S", lambda e, b: e.dma_start(x1[:, :, :], out_v[b]),
               after=[("r_o", PREV)], done=("ra", "r_acc"), carrier=True)
            for x_ in range(NE):
                prev = (f"r_s{x_ - 1}", 0) if x_ else (f"r_s{NE - 1}", PREV)
                for k in range(KD):
                    op("T", lambda e, b, k=k, x_=x_: e.matmul(PA[:, :], wr1[:, x_, k, :], xnT[:, k, :],
                                                              start=(k == 0), stop=(k == KD - 1)),
                       after=[("r_x", 0), prev] if k == 0 else (),
                       done=("rt", f"r_h{x_}_mm") if k == KD - 1 else None)
                op("A", lambda e, b: e.activation(hT[:, :], PA[:, :], ACT.Relu),
                   after=[(f"r_h{x_}_mm", 0), (f"r_y{x_ - 1}_mm1", 0) if x_ else (f"r_y{NE - 1}_mm1", PREV)],
                   done=("rs", f"r_r{x_}"))
                op("A", lambda e, b: e.activation(hT[:, :], hT[:, :], ACT.Square),
                   after=[(f"r_r{x_}", 0)], done=("rs", f"r_s{x_}"))
                for k in range(2):
                    for t2 in range(2):
                        t = 2 * k + t2
                        op("T", lambda e, b, t=t, t2=t2, k=k, x_=x_: e.matmul(
                            Y[k][:, t2 * DM:(t2 + 1) * DM], hT[:, t * P:(t + 1) * P], wr2[:, x_, :],
                            start=True, stop=True),
                           after=[(f"r_s{x_}", 0), (f"r_acc{x_ - 1}_{2 * k + 1}", 0) if x_ else
                                  (f"r_acc{NE - 1}_{2 * k + 1}", PREV)] if t2 == 0 else (),
                           done=("rt", f"r_y{x_}_mm{k}") if t2 else None)
                for t in range(TB):
                    op("V", lambda e, b, t=t, x_=x_: e.scalar_tensor_tensor(
                        out=x1[:, t, :], in0=Y[t // 2][:, (t % 2) * DM:(t % 2 + 1) * DM],
                        scalar=pq[:, t, x_:x_ + 1], in1=x1[:, t, :], op0=ALU.mult, op1=ALU.add),
                       after=([("r_pq", 0), ("r_acc", 0)] if x_ == 0 and t == 0 else []) +
                       [(f"r_y{x_}_mm{t // 2}", 0)] + ([(f"r_acc{x_ - 1}_{t}", 0)] if x_ else []),
                       done=("rv", f"r_acc{x_}_{t}"))
            op("S", lambda e, b: e.dma_start(out_v[b], x1[:, :, :]),
               after=[(f"r_acc{NE - 1}_{TB - 1}", 0)], done=("ro", "r_o"), carrier=True)

        first, middle, last = {}, {}, {}
        q = first
        prologue()
        half(0, True, False, True)
        half(1, True, True, True)
        q = middle
        half(0, True, True, True)
        half(1, True, True, True)
        q = last
        half(0, True, True, False)
        half(1, False, True, False)
        epilogue()

        routed_q = {}
        q = routed_q
        routed()

        def run_routed(e, name):
            e.wait_ge(s_f, 3)
            some = e.value_load(flag[0:1, 0:1], min_val=0, max_val=1)
            with e.If(some > 0):
                if name == "S":
                    e.wait_ge(T["qo"].sem, 16 * NQ)
                    e.wait_ge(T["q2"].sem, 16 * NQ)
                    e.wait_ge(T["hc"].sem, STEPS * NQ)
                    e.dma_start(wr1, W1.rearrange("e (k p) f -> p e k f", p=P)).then_inc(s_rw, 16)
                    e.dma_start(wr2, W2.rearrange("e f d -> f e d")).then_inc(s_rw, 16)
                if name == "T":
                    e.wait_ge(s_rw, 32)
                for f in routed_q.get(name, ()):
                    f(e, 0)
                with e.Fori(1, NQ) as c:
                    for f in routed_q.get(name, ()):
                        f(e, c)
                if name == "S":
                    e.wait_ge(T["ro"].sem, 16 * NQ)

        def run(e, name):
            for f in first.get(name, ()):
                f(e, 0)
            with e.Fori(1, NB - 1) as b:
                for f in middle.get(name, ()):
                    f(e, b)
            for f in last.get(name, ()):
                f(e, NB - 1)

        block = ctx.enter_context(nc.Block())
        loads = [
            (w_in[:, :, :], in_wT.rearrange("(k p) e -> p k e", p=P)),
            (w_conv[:, :, :], conv_w.rearrange("(g p) o k -> p g (o k)", p=P)),
            (w_x[:, :, :], x_wT.rearrange("(g p) f -> p g f", p=P)),
            (w_dt[0:R, :], dt_wT),
            (b_dt[:, :], dt_b.rearrange("(g p) -> p g", p=P)),
            (a_log[:, :, :], A_log.rearrange("(g p) n -> p g n", p=P)),
            (d_skip[:, :], D.rearrange("(g p) -> p g", p=P)),
            (w_out[:, :, :], out_wT.rearrange("(g p) d -> p g d", p=P)),
            (w_s1[:, :, :], Ws1.rearrange("(k p) f -> p k f", p=P)),
            (w_s2[:, :], Ws2),
            (w_r[:, :, :], Wr.rearrange("(k p) e -> p k e", p=P)),
        ]

        @block.sync
        def _(e):
            for dst, src in loads:
                e.dma_start(dst, src, allow_slow_non_contiguous=len(dst.shape) == 2).then_inc(s_w, 16)
            run(e, "S")
            run_routed(e, "S")
            e.wait_ge(T["qo"].sem, 16 * NQ)
            e.wait_ge(T["q2"].sem, 16 * NQ)

        @block.gpsimd
        def _(e):
            e.memset(ident[:, :], 0.0).then_inc(s_g, 1)
            e.memset(sel[:, :, :], 0.0).then_inc(s_g, 1)
            e.memset(halo0[:, :, :], 0.0).then_inc(s_g, 1)
            e.memset(mhalf[:, :], -0.5).then_inc(s_g, 1)
            e.wait_ge(s_g, 4)
            e.affine_select(out=ident[:, :], in_=ident[:, :], compare_op=ALU.not_equal, fill=1.0, base=0,
                            pattern=[[-1, P]], channel_multiplier=1).then_inc(s_g, 1)
            for j in range(3):
                if j:
                    e.wait_ge(s_g, 5 + j)
                e.affine_select(out=sel[:, :, :], in_=sel[:, :, :], compare_op=ALU.not_equal, fill=1.0,
                                base=-32 * j, pattern=[[-1, N], [0, P]], channel_multiplier=1).then_inc(s_g, 1)
            e.wait_ge(s_g, 8)
            run(e, "G")

        @block.vector
        def _(e):
            e.wait_ge(s_g, 8)
            e.wait_ge(s_w, 16 * len(loads))
            e.memset(w_dt[R:FX, :], 0.0).then_inc(s_v0, 1)
            for g in range(G):
                for k in range(K):
                    e.tensor_scalar(w_diag[:, g, k, :], ident[:, :], w_conv[:, g, k:k + 1], None,
                                    ALU.mult).then_inc(s_v0, 1)
                e.tensor_scalar(d_diag[:, g, :], ident[:, :], d_skip[:, g:g + 1], None, ALU.mult).then_inc(s_v0, 1)
            e.wait_ge(s_a0, 1)
            e.tensor_scalar(a_neg[:, :, :], a_neg[:, :, :], -1.0, None, ALU.mult).then_inc(s_v0, 1)
            e.memset(ones[:, :], 1.0).then_inc(s_v0, 1)
            run(e, "V")
            last_prob = T["qv"].value(("prob", 1), NB - 1)
            e.wait_ge(T["qv"].sem, last_prob)
            e.tensor_reduce(any_p[:, :], prob[:, :, :, :].rearrange("p q t n -> p (q t n)"),
                            mybir.AxisListType.X, ALU.max).then_inc(s_f, 1)
            e.wait_ge(s_f, 2)
            e.tensor_scalar(flag[:, :], PA[0:1, 0:1], 1.0, None, ALU.min).then_inc(s_f, 1)
            run_routed(e, "V")

        @block.scalar
        def _(e):
            e.wait_ge(s_g, 8)
            e.wait_ge(s_w, 16 * len(loads))
            e.activation(a_neg[:, :, :], a_log[:, :, :], ACT.Exp).then_inc(s_a0, 1)
            e.wait_ge(s_v0, G * (K + 1) + 2)
            run(e, "A")
            run_routed(e, "A")

        @block.tensor
        def _(e):
            e.wait_ge(s_g, 8)
            e.wait_ge(s_w, 16 * len(loads))
            e.wait_ge(s_v0, G * (K + 1) + 1)
            run(e, "T")
            e.wait_ge(s_f, 1)
            e.matmul(PA[0:1, 0:1], any_p[:, :], ones[:, :], start=True, stop=True).then_inc(s_f, 1)
            run_routed(e, "T")


_INS = [("x", "L0_attn_x", None), ("in_wT", "L0_attn_in_proj_w", (1, 0)), ("conv_w", "L0_attn_conv_w", None),
        ("x_wT", "L0_attn_x_proj_w", (1, 0)), ("dt_wT", "L0_attn_dt_proj_w", (1, 0)),
        ("dt_b", "L0_attn_dt_proj_b", None), ("A_log", "L0_attn_A_log", None), ("D", "L0_attn_D", None),
        ("out_wT", "L0_attn_out_proj_w", (1, 0)), ("Ws1", "L0_ffn_Ws1", None), ("Ws2", "L0_ffn_Ws2", None),
        ("W1", "L0_ffn_W1", None), ("W2", "L0_ffn_W2", None), ("Wr", "L0_ffn_Wr", None)]


def kernel(**inputs):
    import numpy as _np
    import concourse.bacc as _bacc
    from concourse import mybir as _mybir
    from concourse.bass_utils import run_bass_kernel_spmd as _run

    nc = _bacc.Bacc("TRN2", target_bir_lowering=False, num_devices=1)
    arrays, args = {}, {}
    for name, source, order in _INS:
        a = _np.asarray(inputs[source])
        a = _np.ascontiguousarray(a if order is None else a.transpose(order))
        arrays[f"in_{name}"] = a
        args[name] = nc.dram_tensor(f"in_{name}", a.shape, _mybir.dt.from_np(a.dtype), kind="ExternalInput").ap()
    shape = inputs["L0_attn_x"].shape
    out = nc.dram_tensor("out_0", tuple(shape), _mybir.dt.float32, kind="ExternalOutput").ap()
    mamba_moe(nc, out=out, **args)
    r = _run(nc, [arrays], core_ids=[0])
    return r.results[0]["out_0"]
```

```python
from contextlib import ExitStack

import concourse.bass as bass
from concourse import mybir

F32 = mybir.dt.float32
BF16 = mybir.dt.bfloat16
I32 = mybir.dt.int32
ALU = mybir.AluOpType
ACT = mybir.ActivationFunctionType

P = 128
CH = 512
EPS = 1e-5
HR = 3
LAG = 2
DR = 4


class Track:

    def __init__(self, sem, amount=1):
        self.sem, self.amount, self.names, self.at = sem, amount, {}, 0
        self.closed = False

    def mark(self, name):
        if name in self.names:
            if self.names[name] == 1:
                self.closed = True
                self.at = 0
            assert self.names[name] == self.at + 1, (name, self.names[name], self.at)
        else:
            assert not self.closed, name
            self.names[name] = self.at + 1
        self.at += 1

    def value(self, name, seq):
        if isinstance(seq, int) and seq < 0:
            return None
        return (seq * len(self.names) + self.names[name]) * self.amount


def mamba_moe(nc, x, in_wT, conv_w, x_wT, dt_wT, dt_b, A_log, D, out_wT, Ws1, Ws2, W1, W2, Wr, out):
    NB, L, DM = x.shape
    ED = out_wT.shape[0]
    N = A_log.shape[1]
    K = conv_w.shape[2]
    R = dt_wT.shape[0]
    F = Ws1.shape[1]
    NE = Wr.shape[1]
    G = ED // P
    KD = DM // P
    TB = CH // P
    HV = L // CH
    NQ = NB * HV
    FX = R + 2 * N
    NG2 = G // 2
    STEPS = NG2 * N
    assert HV == 2 and KD == 2 and FX == 96 and N == 16 and F == P

    x_v = x.rearrange("b (h t p) d -> (b h) p t d", h=HV, p=P)
    out_v = out.rearrange("b (h t p) d -> (b h) p t d", h=HV, p=P)
    c_dram = nc.dram_tensor("c_scratch", (HV, N, CH), F32, kind="Internal").ap()
    x2_dram = nc.dram_tensor("x2_scratch", (NQ, P, KD, CH), F32, kind="Internal").ap()

    with ExitStack() as ctx:
        def sb(name, shape, dt=F32):
            return ctx.enter_context(nc.sbuf_tensor(name, shape, dt))

        def pb(name):
            return ctx.enter_context(nc.psum_tensor(name, [P, 512], F32))

        def sem(name):
            return ctx.enter_context(nc.semaphore(name))

        w_in = sb("w_in", [P, KD, 2 * ED])
        w_conv = sb("w_conv", [P, G, K])
        w_diag = sb("w_diag", [P, G, K, P])
        w_x = sb("w_x", [P, G, FX])
        w_dt = sb("w_dt", [FX, ED])
        b_dt = sb("b_dt", [P, G])
        a_log = sb("a_log", [P, G, N])
        a_neg = sb("a_neg", [P, G, N])
        d_skip = sb("d_skip", [P, G])
        w_out = sb("w_out", [P, G, DM])
        w_s1 = sb("w_s1", [P, KD, F])
        w_s2 = sb("w_s2", [P, DM])
        w_r = sb("w_r", [P, KD, NE])
        ident = sb("ident", [P, P])
        sel = sb("sel", [FX, N, P], BF16)
        mhalf = sb("mhalf", [P, TB])
        xt = sb("xt", [P, TB, DM])
        st = sb("st", [P, TB, 6])
        mv = sb("mv", [P, TB, 2])
        ve = sb("ve", [P, TB])
        rstd = sb("rstd", [P, TB])
        shift = sb("shift", [P, TB])
        xnT = sb("xnT", [P, KD, CH])
        xp = sb("xp", [P, G, K - 1 + CH])
        xc = [sb(f"xc{h}", [P, G, CH]) for h in range(HV)]
        gate = [sb(f"gate{h}", [P, TB, ED]) for h in range(HV)]
        delta = [sb(f"delta{h}", [P, G, CH]) for h in range(HV)]
        u = [sb(f"u{h}", [P, G, CH]) for h in range(HV)]
        dbc = sb("dbc", [FX, CH])
        xt_flat = xt[:, :, :].rearrange("p t d -> p (t d)")
        bc_r = xt_flat[0:FX, 0:CH]
        bc_hi = xt_flat[0:FX, CH:CH + CH // 2].bitcast(BF16)
        bc_mid = xt_flat[0:FX, CH + CH // 2:2 * CH].bitcast(BF16)
        bc3 = [sb(f"bc3_{h}", [FX, CH], BF16) for h in range(HV)]
        cb = sb("cb", [P, N, CH])
        bx = [sb(f"bx{i}", [P, 2, CH]) for i in range(2)]
        hs = [sb(f"hs{i}", [P, 2, CH]) for i in range(HR)]
        hc = [sb(f"hc{i}", [P, 2, CH]) for i in range(HR)]
        hlast = sb("hlast", [P, STEPS, 2])
        ygT = sb("ygT", [P, G, CH])
        x1 = sb("x1", [P, TB, DM])
        st2 = sb("st2", [P, TB, 6])
        mv2 = sb("mv2", [P, TB, 2])
        ve2 = sb("ve2", [P, TB])
        rstd2 = sb("rstd2", [P, TB])
        shift2 = sb("shift2", [P, TB])
        ygT_flat = ygT[:, :, :].rearrange("p g t -> p (g t)")
        x2n = ygT_flat[:, 0:TB * DM].rearrange("p (t d) -> p t d", t=TB)
        x2T = ygT_flat[:, TB * DM:TB * DM + KD * CH].rearrange("p (k t) -> p k t", k=KD)
        hT = ygT_flat[:, 0:CH]
        lg = sb("lg", [P, TB, NE])
        top8 = sb("top8", [P, TB, 8])
        gap = sb("gap", [P, TB])
        p_top = sb("p_top", [P, TB])
        is_top = sb("is_top", [P, TB, NE])
        prob = sb("prob", [P, NQ, TB, NE])
        any_p = sb("any_p", [P, 1])
        ones = sb("ones", [P, 1])
        flag = sb("flag", [1, 1], I32)
        Y = [pb("Y0"), pb("Y1")]
        BB = [pb("BB0"), pb("BB1")]
        DA = [[pb("DA0"), pb("DA1")]] + [[sb(f"da{i}_{g}", [P, CH]) for g in range(2)] for i in range(1, DR)]
        PA, PB = pb("PA"), pb("PB")

        s_win = sem("s_win")
        s_w = sem("s_w")
        s_g = sem("s_g")
        s_sel = sem("s_sel")
        s_v0 = sem("s_v0")
        s_a0 = sem("s_a0")
        T = {
            "bb": Track(sem("m_bb")), "da": Track(sem("m_da")), "bx": Track(sem("m_bx")),
            "sc": Track(sem("m_sc")), "hl": Track(sem("m_hl")), "hc": Track(sem("m_hc")),
            "y": Track(sem("m_y")), "y0": Track(sem("m_y0")), "yg": Track(sem("m_yg")),
            "px": Track(sem("p_x"), 16), "pt": Track(sem("p_t")), "pv": Track(sem("p_v")),
            "pa": Track(sem("p_a")), "pg": Track(sem("p_g")),
            "zt": Track(sem("z_t")), "za": Track(sem("z_a")),
            "pv2": Track(sem("p_v2")), "pa2": Track(sem("p_a2")),
            "pc": Track(sem("p_c"), 16), "cb": Track(sem("p_cb"), 16),
            "qx": Track(sem("q_x"), 16), "qt": Track(sem("q_t")), "qv": Track(sem("q_v")),
            "qa": Track(sem("q_a")), "ot": Track(sem("o_t")), "oa": Track(sem("o_a")),
            "ov": Track(sem("o_v")), "og": Track(sem("o_g")), "qo": Track(sem("q_o"), 16),
            "q2": Track(sem("q_x2"), 16),
            "ri": Track(sem("r_in"), 16), "ra": Track(sem("r_acc"), 16), "ro": Track(sem("r_out"), 16),
            "rt": Track(sem("r_t")), "rs": Track(sem("r_a")), "rv": Track(sem("r_v")),
        }
        where = {}
        q = None
        s_carry = {"V": sem("carry_v"), "G": sem("carry_g"), "S": sem("carry_s")}

        def op(engine, make, after=(), done=None, r=0, carrier=False):
            if done:
                T[done[0]].mark((done[1], r % HV))
                where[done[1]] = T[done[0]]

            def run(e, b):
                for name, c in after:
                    track = where[name]
                    v = track.value((name, c % HV), b + c // HV)
                    if v is not None:
                        e.wait_ge(track.sem, v)
                        if engine == "S" and not isinstance(v, int):
                            e.sem_inc(s_carry[engine], 1)
                if carrier and engine != "S" and after and not isinstance(b, int):
                    e.sem_inc(s_carry[engine], 1)
                ins = make(e, b)
                if done:
                    ins.then_inc(T[done[0]].sem, T[done[0]].amount)
            q.setdefault(engine, []).append(run)

        deferred = []

        def later(f):
            deferred.append(f)

        def flush():
            while deferred:
                deferred.pop(0)()

        THROUGH_PA = ["p_trc0", "p_trc1"] + [f"xp{g}" for g in range(G)] + [f"cv{g}" for g in range(G)] + \
            ["dbc"] + [f"sp{g}" for g in range(G)] + [f"z{t}" for t in range(TB)]
        THROUGH_PB = [f"yt{g}" for g in range(G)] + ["x1_0", "x1_1", "o_trc0", "o_trc1", "lg", "hr", "o0", "o1"]
        wide = {"PA": None, "PB": None}

        def bank_of(which, name, r):
            through, bank = (THROUGH_PA, PA) if which == "PA" else (THROUGH_PB, PB)
            i = through.index(name)
            if wide[which]:
                n = len(wide[which])
                if i >= n:
                    return wide[which][i % n], [(through[i - n], r)]
                return wide[which][i], [(f"bx{STEPS - 1}", r), (through[-1], r - 1)] if which == "PB" else []
            return bank, [(through[i - 1], r) if i else (through[-1], r - 1)]

        def chunk(b, r):
            return b * HV + r

        def norm_stats(pre, r, src, stt, mvt, vet, rt, sh, ready):
            tv, tg = pre + "v", pre + "g"
            for t in range(TB):
                op("V", lambda e, b, t=t: e.bn_stats(stt[:, t, :], src[:, t, :]),
                   after=ready if t == 0 else (), done=(tv, f"{pre}_st{t}"), r=r)
            for t in range(TB):
                w = [(f"{pre}_st{t}", r)]
                if t == 0:
                    w.append((f"{pre}_shift", r - 1))
                op("V", lambda e, b, t=t: e.bn_aggr(mvt[:, t, :], stt[:, t, :]),
                   after=w, done=(tv, f"{pre}_mv{t}"), r=r, carrier=True)
            op("G", lambda e, b: e.tensor_scalar(vet[:, :], mvt[:, :, 1], EPS, None, ALU.add),
               after=[(f"{pre}_mv{TB - 1}", r), (f"{pre}_rstd", r - 1)], done=(tg, f"{pre}_ve"), r=r, carrier=True)
            op("G", lambda e, b: e.tensor_tensor(rt[:, :], vet[:, :], mhalf[:, :], ALU.pow),
               after=[(f"{pre}_ve", r), (f"{pre}_n{TB - 1}", r - 1)], done=(tg, f"{pre}_rstd"), r=r)

            op("G", lambda e, b: e.tensor_scalar(sh[:, :], mvt[:, :, 0], -1.0, None, ALU.mult),
               after=[(f"{pre}_n{TB - 1}", r - 1)], done=(tg, f"{pre}_neg"), r=r, carrier=True)
            op("G", lambda e, b: e.tensor_tensor(sh[:, :], sh[:, :], rt[:, :], ALU.mult),
               after=[(f"{pre}_neg", r), (f"{pre}_rstd", r)], done=(tg, f"{pre}_shift"), r=r)

        def norm_apply(pre, r, src, dst, rt, sh, freed):
            for t in range(TB):
                op("A", lambda e, b, t=t: e.activation(
                    dst[:, t, :], src[:, t, :], ACT.Identity, bias=sh[:, t:t + 1], scale=rt[:, t:t + 1]),
                   after=([(f"{pre}_shift", r)] + freed) if t == 0 else (), done=(pre + "a", f"{pre}_n{t}"), r=r)

        def transposed(pre, k, r, src, dst, which, freed):
            bank, free = bank_of(which, f"{pre}_trc{k}", r)
            for t in range(TB):
                op("T", lambda e, b, t=t: e.transpose(
                    bank[:, t * P:(t + 1) * P], src[:, t, k * P:(k + 1) * P], ident[:, :]),
                   after=[(f"{pre}_n{t}", r)] + (free if t == 0 else []),
                   done=(pre + "t", f"{pre}_tr{k}") if t == TB - 1 else None, r=r)
            later(lambda: op("A", lambda e, b: e.activation(dst[:, k, :], bank[:, :], ACT.Copy),
                             after=[(f"{pre}_tr{k}", r)] + freed, done=(pre + "a", f"{pre}_trc{k}"), r=r))

        def prep_load(r):
            op("S", lambda e, b: e.dma_start(xt[:, :, :], x_v[chunk(b, r)]),
               after=[("b_lo", r - 1), ("b_mid0", r - 1)], done=("px", "x"), r=r, carrier=True)

        def prep_stats(r):
            norm_stats("p", r, xt, st, mv, ve, rstd, shift, [("x", r)])

        def prep_norm(r):
            norm_apply("p", r, xt, xt, rstd, shift, [])

        def prep_transpose(r, k):
            transposed("p", k, r, xt, xnT, "PA", [("z3_mm", r - 1)])

        def prep_halo(r):
            halo = xp[:, :, 0:K - 1]
            if r % HV == 0:
                op("A", lambda e, b: e.activation(
                    halo, halo0[:, :, :], ACT.Copy),
                   after=[("cv3_mm", r - 1), ("halo", r - 1)], done=("pa", "halo"), r=r)
            else:
                op("A", lambda e, b: e.activation(halo, xp[:, :, CH:CH + K - 1], ACT.Copy),
                   after=[("cv3_mm", r - 1), ("xp3", r - 1)], done=("pa", "halo"), r=r)

        def prep_in(r, g):
            bank, free = bank_of("PA", f"xp{g}", r)
            for k in range(KD):
                op("T", lambda e, b, k=k: e.matmul(bank[:, :], w_in[:, k, g * P:(g + 1) * P], xnT[:, k, :],
                                                   start=(k == 0), stop=(k == KD - 1)),
                   after=[("p_trc1", r)] + free if k == 0 else (),
                   done=("pt", f"xp{g}_mm") if k == KD - 1 else None, r=r)
            later(lambda: op("A", lambda e, b: e.activation(xp[:, g, K - 1:], bank[:, :], ACT.Copy),
                             after=[(f"xp{g}_mm", r), ("halo", r)], done=("pa", f"xp{g}"), r=r))

        def prep_z(r, t):
            bank, free = bank_of("PA", f"z{t}", r)
            for k in range(KD):
                op("T", lambda e, b, k=k: e.matmul(
                    bank[:, :], xnT[:, k, t * P:(t + 1) * P], w_in[:, k, ED:2 * ED],
                    start=(k == 0), stop=(k == KD - 1)),
                   after=free if k == 0 else (),
                   done=("zt", f"z{t}_mm") if k == KD - 1 else None, r=r)
            later(lambda: op("A", lambda e, b: e.activation(gate[r % HV][:, t, :], bank[:, :], ACT.Copy),
                             after=[(f"z{t}_mm", r), ("yt3_mm", r - 2)], done=("za", f"z{t}"), r=r))

        def prep_conv(r, g, part):
            bank, free = bank_of("PA", f"cv{g}", r)
            for k in range(part * K // 2, (part + 1) * K // 2):
                op("T", lambda e, b, k=k: e.matmul(bank[:, :], w_diag[:, g, k, :], xp[:, g, k:k + CH],
                                                   start=(k == 0), stop=(k == K - 1)),
                   after=[(f"xp{g}", r)] + free if k == 0 else (),
                   done=("pt", f"cv{g}_mm") if k == K - 1 else None, r=r)
            if part:
                later(lambda: op("A", lambda e, b: e.activation(xc[r % HV][:, g, :], bank[:, :], ACT.Copy),
                                 after=[(f"cv{g}_mm", r), ("dx1", r - 2)], done=("pa", f"cv{g}"), r=r))

        def prep_silu(r):
            h = r % HV
            op("A", lambda e, b: e.activation(xc[h][:, :, :], xc[h][:, :, :], ACT.Silu),
               after=[("cv3", r)], done=("pa", "xc"), r=r)

        def gate_silu(r):
            h = r % HV
            op("A", lambda e, b: e.activation(gate[h][:, :, :], gate[h][:, :, :], ACT.Silu),
               after=[("z3", r)], done=("pa2", "gate"), r=r)

        def prep_x_mm(r, part):
            h = r % HV
            bank, free = bank_of("PA", "dbc", r)
            for g in range(part * G // 2, (part + 1) * G // 2):
                op("T", lambda e, b, g=g: e.matmul(bank[0:FX, :], w_x[:, g, :], xc[h][:, g, :],
                                                   start=(g == 0), stop=(g == G - 1)),
                   after=[("xc", r)] + free if g == 0 else (),
                   done=("pt", "xw_mm") if g == G - 1 else None, r=r)

        lo, hi = FX - 2 * N, FX

        def prep_x_out(r):
            h = r % HV
            bank, _ = bank_of("PA", "dbc", r)
            op("A", lambda e, b: e.activation(dbc[:, :], bank[0:FX, :], ACT.Copy),
               after=[("xw_mm", r), ("dt3_mm", r - 1), ("b_r", r - 1), ("c_out", r - 1)],
               done=("pa", "dbc"), r=r)
            op("S", lambda e, b: e.dma_start(c_dram[h], dbc[R + N:FX, :]),
               after=[("dbc", r), (f"cb{N // 4 - 1}", r - 2)], done=("pc", "c_out"), r=r)
            op("A", lambda e, b: e.activation(bc_hi[lo:hi, :], dbc[lo:hi, :], ACT.Copy),
               after=[("dbc", r), ("p_tr1", r)], done=("pa", "b_hi"), r=r)
            op("A", lambda e, b: e.activation(bc3[h][0:32, :], dbc[lo:hi, :], ACT.Copy),
               after=[(f"bb{STEPS - 1}", r - 2)], done=("pa", "b_hi0"), r=r)

        def prep_b_rest(r):
            op("V", lambda e, b: e.tensor_tensor(bc_r[lo:hi, :], dbc[lo:hi, :], bc_hi[lo:hi, :], ALU.subtract),
               after=[("b_hi", r), ("b_mid0", r - 1)], done=("pv", "b_r"), r=r)

        def prep_b_mid(r):
            h = r % HV
            op("A", lambda e, b: e.activation(bc_mid[lo:hi, :], bc_r[lo:hi, :], ACT.Copy),
               after=[("b_r", r)], done=("pa", "b_mid"), r=r)
            op("A", lambda e, b: e.activation(bc3[h][32:64, :], bc_r[lo:hi, :], ACT.Copy),
               after=(), done=("pa", "b_mid0"), r=r)

        def prep_b_low(r):
            h = r % HV
            op("V", lambda e, b: e.tensor_tensor(bc3[h][lo:hi, :], bc_r[lo:hi, :], bc_mid[lo:hi, :], ALU.subtract),
               after=[("b_mid", r), (f"bb{STEPS - 1}", r - 2)], done=("pv", "b_lo"), r=r)

        def prep_dt(r, g):
            h = r % HV
            bank, free = bank_of("PA", f"sp{g}", r)
            op("T", lambda e, b: e.matmul(bank[:, :], w_dt[:, g * P:(g + 1) * P], dbc[:, :], start=True, stop=True),
               after=[("dbc", r)] + free, done=("pt", f"dt{g}_mm"), r=r)
            op("A", lambda e, b: e.activation(delta[h][:, g, :], bank[:, :], ACT.Identity, bias=b_dt[:, g:g + 1]),
               after=[(f"dt{g}_mm", r), (f"da{STEPS - 1}_1", r - 2), ("u1", r - 2)], done=("pa", f"dt{g}"), r=r)
            op("A", lambda e, b: e.activation(u[h][:, g, :], bank[:, :], ACT.Abs, bias=b_dt[:, g:g + 1]),
               after=[(f"bx{STEPS - 1}", r - 2)], done=("pa", f"sp{g}"), r=r)

        def prep_softplus(r, part):
            h = r % HV
            if part == 0:
                op("A", lambda e, b: e.activation(u[h][:, :, :], u[h][:, :, :], ACT.Exp, scale=-1.0),
                   after=[(f"sp{G - 1}", r)], done=("pa", "se"), r=r)
            else:
                op("A", lambda e, b: e.activation(u[h][:, :, :], u[h][:, :, :], ACT.Ln, bias=1.0),
                   after=[("se", r)], done=("pa", "sl"), r=r)

        def prep_delta(r, pair):
            h = r % HV
            pr = slice(2 * pair, 2 * pair + 2)
            tv = "pv2" if pair else "pv"
            op("V", lambda e, b: e.scalar_tensor_tensor(
                out=delta[h][:, pr, :], in0=delta[h][:, pr, :], scalar=0.0, in1=u[h][:, pr, :],
                op0=ALU.max, op1=ALU.add),
               after=[("sl", r)], done=(tv, f"delta{pair}"), r=r)

        def prep_u(r, pair):
            h = r % HV
            pr = slice(2 * pair, 2 * pair + 2)
            tv, ta = ("pv2", "pa2") if pair else ("pv", "pa")
            op("V", lambda e, b: e.tensor_tensor(u[h][:, pr, :], delta[h][:, pr, :], xc[h][:, pr, :], ALU.mult),
               after=[(f"delta{pair}", r), ("xc", r)], done=(tv, f"u{pair}"), r=r)
            for g in (2 * pair, 2 * pair + 1):
                later(lambda g=g: op("A", lambda e, b: e.activation(
                    xc[h][:, g, :], xc[h][:, g, :], ACT.Copy, scale=d_skip[:, g:g + 1]),
                    after=[(f"u{pair}", r), ("xw_mm", r)],
                    done=(ta, f"dxc{pair}" if g % 2 else f"dxc{pair}_"), r=r))

        def prep_cb(r, j):
            h = r % HV
            op("S", lambda e, b: e.dma_start(cb[:, 4 * j:4 * j + 4, :],
                                             c_dram[h, 4 * j:4 * j + 4, :].partition_broadcast(P)),
               after=[("c_out", r), (f"hc{STEPS - N + 4 * j + 3}", r - 1)]
               + ([(f"cb{j - 1}", r)] if j else [(f"cb{N // 4 - 1}", r - 1)]),
               done=("cb", f"cb{j}"), r=r)

        def before(s, r, d):
            s -= d
            return (s, r) if s >= 0 else (s + STEPS, r - 1)

        def after_step(name, s, r, d, tail=""):
            s, r = before(s, r, d)
            return (f"{name}{s}{tail}", r)

        def ring(s, r):
            return (r % HV * STEPS + s) % HR

        def last_user(name, s, r, tail=""):
            at = r % HV * STEPS + s
            seq0 = r - r % HV
            back = at - HR
            if back < 0:
                seq0 -= HV
                back = max(i for i in range(HV * STEPS) if i % HR == at % HR)
            return (f"{name}{back % STEPS}{tail}", seq0 + back // STEPS)

        def main_bcast(s, r):
            op("T", lambda e, b: e.matmul(BB[s % 2][:, :], sel[:, s % N, :], bc3[r % HV][:, :],
                                          start=True, stop=True),
               after=[after_step("bx", s, r, 2)] + ([("b_lo", r), ("b_mid0", r)] if s == 0 else []),
               done=("bb", f"bb{s}"), r=r)

        def main_exp(s, r):
            pair, n = divmod(s, N)
            for g in range(2):
                gg = 2 * pair + g
                op("A", lambda e, b, g=g, gg=gg: e.activation(
                    DA[s % DR][g][:, :], delta[r % HV][:, gg, :], ACT.Exp, scale=a_neg[:, gg, n:n + 1]),
                   after=[after_step("sc", s, r, DR, f"_{g}")] + ([(f"delta{pair}", r)] if n == 0 else []),
                   done=("da", f"da{s}_{g}"), r=r)

        def main_bx(s, r):
            pair, n = divmod(s, N)
            h = r % HV
            op("V", lambda e, b: e.tensor_tensor(
                bx[s % 2][:, :, :], u[h][:, 2 * pair:2 * pair + 2, :],
                BB[s % 2][:, :].rearrange("p (o t) -> p o t", o=1).broadcast_to([P, 2, CH]), ALU.mult),
               after=[(f"bb{s}", r), after_step("sc", s, r, 2, "_1")] + ([(f"u{pair}", r)] if n == 0 else []),
               done=("bx", f"bx{s}"), r=r)

        def main_scan(s, r, g):
            h = r % HV
            first = 0.0 if h == 0 else hlast[:, s, g:g + 1]
            wait = [(f"da{s}_{g}", r)]
            if g == 0:
                wait += [(f"bx{s}", r), last_user("hc", s, r)]
                if h:
                    wait.append((f"hl{s}", r - 1))
            op("V", lambda e, b: e.tensor_tensor_scan(
                hs[ring(s, r)][:, g, :], DA[s % DR][g][:, :], bx[s % 2][:, g, :], first, ALU.mult, ALU.add),
               after=wait, done=("sc", f"sc{s}_{g}"), r=r)

        def main_keep(s, r):
            if r % HV == 0:
                op("V", lambda e, b: e.tensor_copy(hlast[:, s, :], hs[ring(s, r)][:, :, CH - 1]),
                   after=[(f"sc{s}_1", r)], done=("hl", f"hl{s}"), r=r)

        def main_times_c(s, r):
            n = s % N
            op("G", lambda e, b: e.tensor_tensor(
                hc[ring(s, r)][:, :, :], hs[ring(s, r)][:, :, :],
                cb[:, n:n + 1, :].broadcast_to([P, 2, CH]), ALU.mult),
               after=[(f"sc{s}_1", r)] + [last_user("y", s, r)]
               + ([(f"cb{n // 4}", r)] if s < N and n % 4 == 0 else []),
               done=("hc", f"hc{s}"), r=r)

        def y_at(t, g):
            return Y[t // 2][:, (t % 2) * 2 * P + g * P:(t % 2) * 2 * P + (g + 1) * P]

        def main_start(pair, r):
            h = r % HV
            for t in range(TB):
                for g in range(2):
                    w = []
                    if t == 0 and g == 0:
                        w = [("yg0", r) if pair else ("yg1", r - 1), (f"dxc{pair}", r), ("z3", r)]
                    op("T", lambda e, b, t=t, g=g: e.matmul(
                        y_at(t, g), xc[h][:, 2 * pair + g, t * P:(t + 1) * P], ident[:, :], is_transpose=True,
                        start=(t % 2 == 0 and g == 0), stop=False, skip_group_check=True),
                       after=w, done=("y0", f"dx{pair}") if t == TB - 1 and g else None, r=r)

        def main_sum(s, r):
            n = s % N
            for t in range(TB):
                for g in range(2):
                    op("T", lambda e, b, t=t, g=g: e.matmul(
                        y_at(t, g), hc[ring(s, r)][:, g, t * P:(t + 1) * P], ident[:, :], is_transpose=True,
                        start=False, stop=(n == N - 1), skip_group_check=True),
                       after=[(f"hc{s}", r)] if t == 0 and g == 0 else (),
                       done=("y", f"y{s}") if t == TB - 1 and g else None, r=r)

        def post_gate(r, pair):
            h = r % HV
            for k in range(2):
                part = gate[h][:, 2 * k:2 * k + 2, pair * 2 * P:(pair + 1) * 2 * P]
                op("V", lambda e, b, k=k, part=part: e.tensor_tensor(
                    part, part, Y[k][:, :].rearrange("p (t c) -> p t c", t=2), ALU.mult),
                   after=[(f"y{pair * N + N - 1}", r), ("gate", r)] if k == 0 else (),
                   done=("yg", f"yg{pair}" if k else f"yg{pair}_"), r=r)

        def post_back(r, g):
            h = r % HV
            bank, free = bank_of("PB", f"yt{g}", r)
            for t in range(TB):
                op("T", lambda e, b, t=t: e.transpose(bank[:, t * P:(t + 1) * P], gate[h][:, t, g * P:(g + 1) * P],
                                                      ident[:, :]),
                   after=[("yg0", r), ("yg1", r)] + free if t == 0 else (),
                   done=("qt", f"yt{g}_mm") if t == TB - 1 else None, r=r)
            later(lambda: op("A", lambda e, b: e.activation(ygT[:, g, :], bank[:, :], ACT.Copy),
               after=[(f"yt{g}_mm", r), ("x2_out", r - 1), ("o1_mm", r - 1)], done=("qa", f"yt{g}"), r=r))

        def post_load(r):
            op("S", lambda e, b: e.dma_start(x1[:, :, :], x_v[chunk(b, r)]),
               after=[("o", r - 1)], done=("qx", "xr"), r=r, carrier=True)

        def post_out(r, t):
            k, t2 = divmod(t, 2)
            bank, free = bank_of("PB", f"x1_{k}", r)
            for g in range(G):
                w = [("yt3", r)] + free if t2 == 0 and g == 0 else []
                op("T", lambda e, b, g=g: e.matmul(
                    bank[:, t2 * DM:(t2 + 1) * DM], ygT[:, g, t * P:(t + 1) * P], w_out[:, g, :],
                    start=(g == 0), stop=(g == G - 1)),
                   after=w, done=("qt", f"op{k}_mm") if t2 == 1 and g == G - 1 else None, r=r)
            if t2:
                later(lambda: op("V", lambda e, b: e.tensor_tensor(
                    x1[:, 2 * k:2 * k + 2, :], x1[:, 2 * k:2 * k + 2, :],
                    bank[:, :].rearrange("p (t d) -> p t d", t=2), ALU.add),
                    after=[(f"op{k}_mm", r), ("xr", r)], done=("qv", f"x1_{k}"), r=r))

        def post_stats(r):
            norm_stats("o", r, x1, st2, mv2, ve2, rstd2, shift2, [("x1_1", r)])

        def post_norm(r):
            norm_apply("o", r, x1, x2n, rstd2, shift2, [("o_tr1", r - 1), ("op1_mm", r)])

        def post_transpose(r, k):
            transposed("o", k, r, x2n, x2T, "PB", [("h_mm", r - 1), ("x2_out", r - 1)])

        def post_route(r):
            op("S", lambda e, b: e.dma_start(x2_dram[chunk(b, r)], x2T[:, :, :]),
               after=[("o_trc1", r)], done=("q2", "x2_out"), r=r, carrier=True)
            bank, free = bank_of("PB", "lg", r)
            for t in range(TB):
                for k in range(KD):
                    op("T", lambda e, b, t=t, k=k: e.matmul(
                        bank[:, t * NE:(t + 1) * NE], x2T[:, k, t * P:(t + 1) * P], w_r[:, k, :],
                        start=(k == 0), stop=(k == KD - 1)),
                       after=[("o_trc1", r)] + free if t == 0 and k == 0 else (),
                       done=("ot", "lg_mm") if t == TB - 1 and k == KD - 1 else None, r=r)

        def post_top(r):
            bank, _ = bank_of("PB", "lg", r)
            op("V", lambda e, b: e.tensor_copy(lg[:, :, :], bank[:, 0:TB * NE].rearrange("p (t n) -> p t n", t=TB)),
               after=[("lg_mm", r), ("prob", r - 1)], done=("ov", "lg"), r=r)
            for t in range(TB):
                op("V", lambda e, b, t=t: e.max(top8[:, t, :], lg[:, t, :]),
                   after=[("lg", r)] if t == 0 else (), done=("ov", f"top{t}"), r=r, carrier=True)
            op("V", lambda e, b: e.tensor_tensor(gap[:, :], top8[:, :, 1], top8[:, :, 0], ALU.subtract),
               after=[(f"top{TB - 1}", r)], done=("ov", "gap"), r=r)
            op("A", lambda e, b: e.activation(gap[:, :], gap[:, :], ACT.Exp),
               after=[("gap", r)], done=("oa", "gap_e"), r=r)

        def post_prob(r):
            op("V", lambda e, b: e.tensor_scalar(p_top[:, :], gap[:, :], 1.0, None, ALU.add),
               after=[("gap_e", r)], done=("ov", "p_den"), r=r)
            op("V", lambda e, b: e.reciprocal(p_top[:, :], p_top[:, :]),
               after=[("p_den", r)], done=("ov", "p_top"), r=r)
            op("V", lambda e, b: e.tensor_scalar(p_top[:, :], p_top[:, :], 1.0, None, ALU.is_ge),
               after=[("p_top", r)], done=("ov", "p_tr"), r=r)
            op("V", lambda e, b: e.tensor_tensor(
                is_top[:, :, :], lg[:, :, :], top8[:, :, 0:1].broadcast_to([P, TB, NE]), ALU.is_ge),
               done=("ov", "is_top"), r=r)
            op("V", lambda e, b: e.tensor_tensor(
                prob[:, chunk(b, r), :, :] if isinstance(b, int) else
                prob[:, bass.ds(chunk(b, r), 1), :, :].rearrange("p o t n -> p (o t) n"),
                is_top[:, :, :], p_top[:, :].rearrange("p (t o) -> p t o", o=1).broadcast_to([P, TB, NE]), ALU.mult),
               after=[("is_top", r)], done=("ov", "prob"), r=r)

        def post_hidden(r):
            bank, free = bank_of("PB", "hr", r)
            for k in range(KD):
                op("T", lambda e, b, k=k: e.matmul(bank[:, :], w_s1[:, k, :], x2T[:, k, :],
                                                   start=(k == 0), stop=(k == KD - 1)),
                   after=free if k == 0 else (),
                   done=("ot", "h_mm") if k == KD - 1 else None, r=r)

        def post_square(r):
            bank, _ = bank_of("PB", "hr", r)
            op("A", lambda e, b: e.activation(hT[:, :], bank[:, :], ACT.Relu),
               after=[("h_mm", r), ("o1_mm", r - 1)], done=("oa", "hr"), r=r)
            op("A", lambda e, b: e.activation(hT[:, :], hT[:, :], ACT.Square),
               after=[("hr", r)], done=("oa", "h"), r=r)

        def post_shared(r, k):
            bank, free = bank_of("PB", f"o{k}", r)
            for t2 in range(2):
                t = 2 * k + t2
                op("T", lambda e, b, t=t, t2=t2: e.matmul(
                    bank[:, t2 * DM:(t2 + 1) * DM], hT[:, t * P:(t + 1) * P], w_s2[:, :], start=True, stop=True),
                   after=[("h", r)] + free if t2 == 0 else (),
                   done=("ot", f"o{k}_mm") if t2 else None, r=r)
            later(lambda: op("V", lambda e, b: e.tensor_tensor(
                x1[:, 2 * k:2 * k + 2, :], x1[:, 2 * k:2 * k + 2, :],
                bank[:, :].rearrange("p (t d) -> p t d", t=2), ALU.add),
                after=[(f"o{k}_mm", r)], done=("ov", f"o{k}"), r=r))

        def post_store(r):
            op("S", lambda e, b: e.dma_start(out_v[chunk(b, r)], x1[:, :, :]),
               after=[("o1", r)], done=("qo", "o"), r=r, carrier=True)

        pq = sb("pq", [P, TB, NE])
        s_f = sem("s_f")
        s_rw = sem("s_rw")
        halo0 = sb("halo0", [P, G, K - 1])

        loads = [
            (w_conv[:, :, :], conv_w.rearrange("(g p) o k -> p g (o k)", p=P)),
            (a_log[:, :, :], A_log.rearrange("(g p) n -> p g n", p=P)),
            (w_x[:, :, :], x_wT.rearrange("(g p) f -> p g f", p=P)),
            (w_dt[0:R, :], dt_wT),
            (b_dt[:, :], dt_b.rearrange("(g p) -> p g", p=P)),
            (d_skip[:, :], D.rearrange("(g p) -> p g", p=P)),
            (w_out[:, :, :], out_wT.rearrange("(g p) d -> p g d", p=P)),
            (w_s1[:, :, :], Ws1.rearrange("(k p) f -> p k f", p=P)),
            (w_s2[:, :], Ws2),
            (w_r[:, :, :], Wr.rearrange("(k p) e -> p k e", p=P)),
        ]

        def start_loads():
            def run(e, b):
                e.dma_start(w_in[:, :, :], in_wT.rearrange("(k p) e -> p k e", p=P)).then_inc(s_win, 16)
                for dst, src in loads:
                    e.dma_start(dst, src, allow_slow_non_contiguous=len(dst.shape) == 2).then_inc(s_w, 16)
            q["S"].append(run)

        def start_selector():
            def run(e, b):
                e.memset(sel[:, :, :], 0.0).then_inc(s_sel, 1)
                for j in range(3):
                    e.wait_ge(s_sel, 1 + j)
                    e.affine_select(out=sel[:, :, :], in_=sel[:, :, :], compare_op=ALU.not_equal, fill=1.0,
                                    base=-32 * j, pattern=[[-1, N], [0, P]], channel_multiplier=1).then_inc(s_sel, 1)
            q["G"].append(run)

        def start_diagonals(r):
            def scalar(e, b):
                e.wait_ge(s_w, 16 * len(loads))
                e.activation(a_neg[:, :, :], a_log[:, :, :], ACT.Exp).then_inc(s_a0, 1)

            def vector(e, b):
                e.wait_ge(s_w, 16 * len(loads))
                e.memset(w_dt[R:FX, :], 0.0).then_inc(s_v0, 1)
                e.memset(ones[:, :], 1.0).then_inc(s_v0, 1)
                for g in range(G):
                    for k in range(K):
                        e.tensor_scalar(w_diag[:, g, k, :], ident[:, :], w_conv[:, g, k:k + 1], None,
                                        ALU.mult).then_inc(s_v0, 1)
                e.wait_ge(s_a0, 1)
                e.tensor_scalar(a_neg[:, :, :], a_neg[:, :, :], -1.0, None, ALU.mult).then_inc(s_v0, 1)
            q["A"].append(scalar)
            q["V"].append(vector)

        def start_in_wait(r):
            q["T"].append(lambda e, b: e.wait_ge(s_win, 16))

        def start_wait(r):
            def run(e, b):
                e.wait_ge(s_w, 16 * len(loads))
                e.wait_ge(s_v0, G * K + 3)
                e.wait_ge(s_sel, 4)
            q["T"].append(run)
            q["A"].append(run)

        def steps(f, at):
            return [(s, f, i) for i, s in enumerate(at)]

        NEXT2 = [(24, prep_load), (29, prep_stats), (30, prep_norm)]
        PREP = [(0, prep_halo)]
        PREP += steps(prep_transpose, (1, 2))
        PREP += steps(prep_in, (3, 4, 5, 6))
        PREP += [(7 + i, prep_conv, i // 2, i % 2) for i in range(2 * G)]
        PREP += [(15, prep_silu)] + steps(prep_x_mm, (17, 18)) + [(19, prep_x_out)]
        PREP += [(20, prep_b_rest), (21, prep_b_mid), (22, prep_b_low)]
        PREP += steps(prep_dt, (20, 21, 22, 23)) + steps(prep_softplus, (24, 25))
        PREP += steps(prep_cb, (25, 27, 29, 31)) + [(27, prep_delta, 0), (28, prep_u, 0)]
        PREP.sort(key=lambda item: item[0])
        Z = steps(prep_z, (25, 27, 28, 30))
        OWN = [(7, prep_delta, 1), (10, prep_u, 1), (14, gate_silu)]
        POST = [(1, post_gate, 1)] + steps(post_back, (4, 5, 6, 7)) + [(8, post_load)]
        POST += steps(post_out, (15, 19, 21, 24)) + [(25, post_stats), (27, post_norm)]
        POST += steps(post_transpose, (28, 29)) + [(30, post_route), (31, post_top)]
        POST2 = [(0, post_hidden), (1, post_square)] + steps(post_shared, (1, 2))
        POST2 += [(3, post_prob), (3, post_store)]

        def side(s, r, prep, post, post2, load):
            flush()
            for items, r2, wanted in ((POST2, r - 2, post2), (POST, r - 1, post), (PREP, r + 1, prep), (Z, r + 1, prep),
                                      (OWN, r, True), (NEXT2, r + 2, load)):
                for at, f, *args in items:
                    if wanted and at == s:
                        f(r2, *args)
            if s == N + LAG - 1:
                post_gate(r, 0)
            if s == STEPS - 1:
                flush()

        def half(r, prep, post, post2, load):
            for s in range(STEPS):
                def step(d):
                    return (s + d, r) if s + d < STEPS else (s + d - STEPS, r + 1)

                if s + 2 < STEPS or prep:
                    main_bcast(*step(2))
                if s + DR - 1 < STEPS or prep:
                    main_exp(*step(DR - 1))
                main_scan(s, r, 0)
                if s or r % HV:
                    main_keep(*before(s, r, 1))
                if s + 1 < STEPS or prep:
                    main_bx(*step(1))
                main_scan(s, r, 1)
                main_times_c(s, r)
                if s >= LAG or post:
                    ps, pr_ = before(s, r, LAG)
                    if ps % N == 0:
                        main_start(ps // N, r)
                    main_sum(ps, pr_)
                side(s, r, prep, post, post2, load)

        def alone(items, r):
            for s in range(STEPS):
                flush()
                for at, f, *args in items:
                    if at == s:
                        f(r, *args)
            flush()

        def prologue():
            prep_load(0)
            start_loads()
            prep_stats(0)
            start_selector()
            wide["PA"] = [PA, PB, Y[0], Y[1]]
            prep_norm(0)
            alone(PREP + [(0, start_diagonals), (1, start_in_wait), (5, start_wait)], 0)
            prep_load(1)
            main_bcast(0, 0)
            main_bcast(1, 0)
            for s in range(DR - 1):
                main_exp(s, 0)
            main_bx(0, 0)
            alone(Z, 0)
            prep_stats(1)
            prep_norm(1)
            wide["PA"] = None

        def epilogue():
            m = HV - 1
            alone(POST2, m - 1)
            for s in range(STEPS - LAG, STEPS):
                main_sum(s, m)
            wide["PB"] = [PB, PA, BB[0], BB[1]]
            alone(POST, m)
            alone(POST2, m)

        wr1 = cb[:, :, :].rearrange("p n t -> p (n t)")[:, 0:NE * KD * F].rearrange(
            "p (e k f) -> p e k f", e=NE, k=KD)
        wr2 = cb[:, :, :].rearrange("p n t -> p (n t)")[:, NE * KD * F:NE * KD * F + NE * DM].rearrange(
            "p (e d) -> p e d", e=NE)
        PREV = -HV

        def routed():
            op("V", lambda e, b: e.tensor_copy(pq[:, :, :], prob[:, b, :, :] if isinstance(b, int) else
                                               prob[:, bass.ds(b, 1), :, :].rearrange("p o t n -> p (o t) n")),
               after=[(f"r_acc{NE - 1}_{TB - 1}", PREV)], done=("rv", "r_pq"))
            op("S", lambda e, b: e.dma_start(xnT[:, :, :], x2_dram[b]),
               after=[(f"r_h{NE - 1}_mm", PREV)], done=("ri", "r_x"), carrier=True)
            op("S", lambda e, b: e.dma_start(x1[:, :, :], out_v[b]),
               after=[("r_o", PREV)], done=("ra", "r_acc"), carrier=True)
            for x_ in range(NE):
                prev = (f"r_s{x_ - 1}", 0) if x_ else (f"r_s{NE - 1}", PREV)
                for k in range(KD):
                    op("T", lambda e, b, k=k, x_=x_: e.matmul(PA[:, :], wr1[:, x_, k, :], xnT[:, k, :],
                                                              start=(k == 0), stop=(k == KD - 1)),
                       after=[("r_x", 0), prev] if k == 0 else (),
                       done=("rt", f"r_h{x_}_mm") if k == KD - 1 else None)
                op("A", lambda e, b: e.activation(hT[:, :], PA[:, :], ACT.Relu),
                   after=[(f"r_h{x_}_mm", 0), (f"r_y{x_ - 1}_mm1", 0) if x_ else (f"r_y{NE - 1}_mm1", PREV)],
                   done=("rs", f"r_r{x_}"))
                op("A", lambda e, b: e.activation(hT[:, :], hT[:, :], ACT.Square),
                   after=[(f"r_r{x_}", 0)], done=("rs", f"r_s{x_}"))
                for k in range(2):
                    for t2 in range(2):
                        t = 2 * k + t2
                        op("T", lambda e, b, t=t, t2=t2, k=k, x_=x_: e.matmul(
                            Y[k][:, t2 * DM:(t2 + 1) * DM], hT[:, t * P:(t + 1) * P], wr2[:, x_, :],
                            start=True, stop=True),
                           after=[(f"r_s{x_}", 0), (f"r_acc{x_ - 1}_{2 * k + 1}", 0) if x_ else
                                  (f"r_acc{NE - 1}_{2 * k + 1}", PREV)] if t2 == 0 else (),
                           done=("rt", f"r_y{x_}_mm{k}") if t2 else None)
                for t in range(TB):
                    op("V", lambda e, b, t=t, x_=x_: e.scalar_tensor_tensor(
                        out=x1[:, t, :], in0=Y[t // 2][:, (t % 2) * DM:(t % 2 + 1) * DM],
                        scalar=pq[:, t, x_:x_ + 1], in1=x1[:, t, :], op0=ALU.mult, op1=ALU.add),
                       after=([("r_pq", 0), ("r_acc", 0)] if x_ == 0 and t == 0 else []) +
                       [(f"r_y{x_}_mm{t // 2}", 0)] + ([(f"r_acc{x_ - 1}_{t}", 0)] if x_ else []),
                       done=("rv", f"r_acc{x_}_{t}"))
            op("S", lambda e, b: e.dma_start(out_v[b], x1[:, :, :]),
               after=[(f"r_acc{NE - 1}_{TB - 1}", 0)], done=("ro", "r_o"), carrier=True)

        first, middle, last = {}, {}, {}
        q = first
        prologue()
        half(0, True, False, False, True)
        half(1, True, True, False, True)
        q = middle
        half(0, True, True, True, True)
        half(1, True, True, True, True)
        q = last
        half(0, True, True, True, False)
        half(1, False, True, True, False)
        epilogue()

        routed_q = {}
        q = routed_q
        routed()

        def run_routed(e, name):
            e.wait_ge(s_f, 3)
            some = e.value_load(flag[0:1, 0:1], min_val=0, max_val=1)
            with e.If(some > 0):
                if name == "S":
                    e.wait_ge(T["qo"].sem, 16 * NQ)
                    e.wait_ge(T["q2"].sem, 16 * NQ)
                    e.wait_ge(T["hc"].sem, STEPS * NQ)
                    e.dma_start(wr1, W1.rearrange("e (k p) f -> p e k f", p=P)).then_inc(s_rw, 16)
                    e.dma_start(wr2, W2.rearrange("e f d -> f e d")).then_inc(s_rw, 16)
                if name == "T":
                    e.wait_ge(s_rw, 32)
                for f in routed_q.get(name, ()):
                    f(e, 0)
                with e.Fori(1, NQ) as c:
                    for f in routed_q.get(name, ()):
                        f(e, c)
                if name == "S":
                    e.wait_ge(T["ro"].sem, 16 * NQ)

        def run(e, name):
            for f in first.get(name, ()):
                f(e, 0)
            with e.Fori(1, NB - 1) as b:
                for f in middle.get(name, ()):
                    f(e, b)
            for f in last.get(name, ()):
                f(e, NB - 1)

        block = ctx.enter_context(nc.Block())
        @block.sync
        def _(e):
            run(e, "S")
            run_routed(e, "S")
            e.wait_ge(T["qo"].sem, 16 * NQ)
            e.wait_ge(T["q2"].sem, 16 * NQ)

        @block.gpsimd
        def _(e):
            e.memset(ident[:, :], 0.0).then_inc(s_g, 1)
            e.memset(halo0[:, :, :], 0.0).then_inc(s_g, 1)
            e.memset(mhalf[:, :], -0.5).then_inc(s_g, 1)
            e.wait_ge(s_g, 3)
            e.affine_select(out=ident[:, :], in_=ident[:, :], compare_op=ALU.not_equal, fill=1.0, base=0,
                            pattern=[[-1, P]], channel_multiplier=1).then_inc(s_g, 1)
            run(e, "G")

        @block.vector
        def _(e):
            e.wait_ge(s_g, 4)
            run(e, "V")
            last_prob = T["ov"].value(("prob", 1), NB - 1)
            e.wait_ge(T["ov"].sem, last_prob)
            e.tensor_reduce(any_p[:, :], prob[:, :, :, :].rearrange("p q t n -> p (q t n)"),
                            mybir.AxisListType.X, ALU.max).then_inc(s_f, 1)
            e.wait_ge(s_f, 2)
            e.tensor_scalar(flag[:, :], PA[0:1, 0:1], 1.0, None, ALU.min).then_inc(s_f, 1)
            run_routed(e, "V")

        @block.scalar
        def _(e):
            e.wait_ge(s_g, 4)
            run(e, "A")
            run_routed(e, "A")

        @block.tensor
        def _(e):
            e.wait_ge(s_g, 4)
            run(e, "T")
            e.wait_ge(s_f, 1)
            e.matmul(PA[0:1, 0:1], any_p[:, :], ones[:, :], start=True, stop=True).then_inc(s_f, 1)
            run_routed(e, "T")


_INS = [("x", "L0_attn_x", None), ("in_wT", "L0_attn_in_proj_w", (1, 0)), ("conv_w", "L0_attn_conv_w", None),
        ("x_wT", "L0_attn_x_proj_w", (1, 0)), ("dt_wT", "L0_attn_dt_proj_w", (1, 0)),
        ("dt_b", "L0_attn_dt_proj_b", None), ("A_log", "L0_attn_A_log", None), ("D", "L0_attn_D", None),
        ("out_wT", "L0_attn_out_proj_w", (1, 0)), ("Ws1", "L0_ffn_Ws1", None), ("Ws2", "L0_ffn_Ws2", None),
        ("W1", "L0_ffn_W1", None), ("W2", "L0_ffn_W2", None), ("Wr", "L0_ffn_Wr", None)]


def kernel(**inputs):
    import numpy as _np
    import concourse.bacc as _bacc
    from concourse import mybir as _mybir
    from concourse.bass_utils import run_bass_kernel_spmd as _run

    nc = _bacc.Bacc("TRN2", target_bir_lowering=False, num_devices=1)
    arrays, args = {}, {}
    for name, source, order in _INS:
        a = _np.asarray(inputs[source])
        a = _np.ascontiguousarray(a if order is None else a.transpose(order))
        arrays[f"in_{name}"] = a
        args[name] = nc.dram_tensor(f"in_{name}", a.shape, _mybir.dt.from_np(a.dtype), kind="ExternalInput").ap()
    shape = inputs["L0_attn_x"].shape
    out = nc.dram_tensor("out_0", tuple(shape), _mybir.dt.float32, kind="ExternalOutput").ap()
    mamba_moe(nc, out=out, **args)
    r = _run(nc, [arrays], core_ids=[0])
    return r.results[0]["out_0"]
```
